# Optimizing a Trainium2 kernel written in Bass

```python
import numpy as np
import jax
import jax.numpy as jnp

def _softmax(x, axis=-1):
    return jax.nn.softmax(x, axis=axis)

def _gelu(x):
    return jax.nn.gelu(x, approximate=True)

def _silu(x):
    return jax.nn.silu(x)

def _sigmoid(x):
    return jax.nn.sigmoid(x)

def _layernorm(x, axis=-1, eps=1e-05):
    m = jnp.mean(x, axis=axis, keepdims=True)
    v = jnp.var(x, axis=axis, keepdims=True)
    return (x - m) / jnp.sqrt(v + eps)

def _scatter_add(tgt, idx, src, axis=0):
    return tgt.at[idx].add(src)

def _segment_sum(src, seg, n):
    return jax.ops.segment_sum(src, seg, n)
kernel_name = 'mk_perceiver_d1_seqx_r8_101271'

def setup_inputs(seed: int=0):
    np.random.seed(seed)
    _w = jnp.asarray

    def _rec_inputs():
        import jax
        import jax.numpy as jnp
        _rk = jax.random.key(seed)
        x = -0.0003929 + 0.9999 * jax.random.normal(jax.random.fold_in(_rk, 1), (2, 128, 256), jnp.float32)
        _lenS = 128 - jax.random.randint(jax.random.fold_in(_rk, 7), (2,), 0, max(1, 128 // 4) + 1, jnp.int32)
        _lenS2 = 2048 - jax.random.randint(jax.random.fold_in(_rk, 8), (2,), 0, max(1, 2048 // 4) + 1, jnp.int32)
        _ctx_2048P = jax.random.normal(jax.random.fold_in(_rk, 11), (2, 16, 256), jnp.float32)
        _ctx_2048c = jax.random.dirichlet(jax.random.fold_in(_rk, 511), 0.3 * jnp.ones((16,), jnp.float32), (2, 2048))
        _ctx_2048t = jnp.einsum('bsk,bkd->bsd', _ctx_2048c, _ctx_2048P)
        _ctx_2048t = _ctx_2048t * jax.lax.rsqrt(jnp.mean(jnp.square(_ctx_2048t)) + 1e-12) * 0.953939
        ctx_2048 = -0.000514642 + 1.00011 * (_ctx_2048t + 0.3 * jax.random.normal(jax.random.fold_in(_rk, 611), (2, 2048, 256), jnp.float32))
        return (x, ctx_2048)
    x, ctx_2048 = _rec_inputs()

    def _L0_xattn_setup():
        import jax, jax.numpy as jnp
        import numpy as np
        DIM = 256
        NHEADS = 32
        HEAD_DIM = DIM // NHEADS
        EPS = 1e-06

        def _rmsnorm(t):
            return t * jax.lax.rsqrt(jnp.mean(t * t, axis=-1, keepdims=True) + EPS)
        key = jax.random.key(seed)
        kx, kc, kq, kk, kv = jax.random.split(key, 5)
        x = jax.random.normal(kx, (2, 512, DIM), dtype=jnp.float32)
        context = jax.random.normal(kc, (2, 64, DIM), dtype=jnp.float32)
        std = 0.02
        Wq = jax.random.normal(kq, (DIM, DIM), dtype=jnp.float32) * std
        Wk = jax.random.normal(kk, (DIM, DIM), dtype=jnp.float32) * std
        Wv = jax.random.normal(kv, (DIM, DIM), dtype=jnp.float32) * std
        return {'x': x, 'context': context, 'Wq': Wq, 'Wk': Wk, 'Wv': Wv}
    _L0_xattn_all = _L0_xattn_setup()
    _L0_xattn_in = {k: v for k, v in _L0_xattn_all.items() if k in ('Wq', 'Wk', 'Wv')}
    del _L0_xattn_all

    def _L0_attn_setup():
        import jax, jax.numpy as jnp
        import numpy as np
        EMB = 256
        HEADS = 16
        key = jax.random.key(seed)
        k_x, k_wqkv, k_bqkv, k_wo, k_bo = jax.random.split(key, 5)
        B, S, E = (2, 256, EMB)
        x = jax.random.normal(k_x, (B, S, E), dtype=jnp.float32)
        W_qkv = jax.random.normal(k_wqkv, (E, 3 * E), dtype=jnp.float32) * 0.02
        b_qkv = jax.random.normal(k_bqkv, (3 * E,), dtype=jnp.float32) * 0.02
        W_out = jax.random.normal(k_wo, (E, E), dtype=jnp.float32) * 0.02
        b_out = jax.random.normal(k_bo, (E,), dtype=jnp.float32) * 0.02
        return {'x': x, 'W_qkv': W_qkv, 'b_qkv': b_qkv, 'W_out': W_out, 'b_out': b_out}
    _L0_attn_all = _L0_attn_setup()
    _L0_attn_in = {k: v for k, v in _L0_attn_all.items() if k in ('W_qkv', 'b_qkv', 'W_out', 'b_out')}
    del _L0_attn_all

    def _L0_ffn_setup():
        import jax, jax.numpy as jnp
        import numpy as np
        HIDDEN = 256
        FFN = 176
        N_EXPERTS = 64
        TOP_K = 6
        N_SHARED = 2
        SHARED_FFN = FFN * N_SHARED
        ROUTED_SCALING = 1.0
        EPS = 1e-20

        def _moe_forward(x, gate_w, w_gate_up, w_down, ws_gate_up, ws_down):
            T = x.shape[0]
            logits = jnp.einsum('th,eh->te', x.astype(jnp.float32), gate_w.astype(jnp.float32))
            scores = jax.nn.softmax(logits, axis=-1)
            topk_w, topk_ids = jax.lax.top_k(scores, TOP_K)
            topk_w = topk_w / (jnp.sum(topk_w, axis=-1, keepdims=True) + EPS)
            topk_w = topk_w * ROUTED_SCALING
            comb = jnp.zeros((T, N_EXPERTS), dtype=x.dtype)
            comb = comb.at[jnp.arange(T)[:, None], topk_ids].add(topk_w.astype(x.dtype))
            gu = jnp.einsum('th,efh->tef', x, w_gate_up)
            g, u = (gu[..., :FFN], gu[..., FFN:])
            act = jax.nn.silu(g) * u
            act = act * comb[:, :, None]
            routed = jnp.einsum('tef,ehf->th', act, w_down)
            sgu = jnp.einsum('th,fh->tf', x, ws_gate_up)
            sg, su = (sgu[..., :SHARED_FFN], sgu[..., SHARED_FFN:])
            shared = jnp.einsum('tf,hf->th', jax.nn.silu(sg) * su, ws_down)
            return routed + shared
        key = jax.random.key(seed)
        k0, k1, k2, k3, k4, k5 = jax.random.split(key, 6)
        hidden_states = jax.random.normal(k0, (1, 32, HIDDEN), dtype=jnp.float32)
        gate_w = jax.random.normal(k1, (N_EXPERTS, HIDDEN), dtype=jnp.float32) * 0.05
        w_gate_up = jax.random.normal(k2, (N_EXPERTS, 2 * FFN, HIDDEN), dtype=jnp.float32) * 0.02
        w_down = jax.random.normal(k3, (N_EXPERTS, HIDDEN, FFN), dtype=jnp.float32) * 0.02
        ws_gate_up = jax.random.normal(k4, (2 * SHARED_FFN, HIDDEN), dtype=jnp.float32) * 0.02
        ws_down = jax.random.normal(k5, (HIDDEN, SHARED_FFN), dtype=jnp.float32) * 0.02
        return {'hidden_states': hidden_states, 'gate_w': gate_w, 'w_gate_up': w_gate_up, 'w_down': w_down, 'ws_gate_up': ws_gate_up, 'ws_down': ws_down}
    _L0_ffn_all = _L0_ffn_setup()
    _L0_ffn_in = {k: v for k, v in _L0_ffn_all.items() if k in ('gate_w', 'w_gate_up', 'w_down', 'ws_gate_up', 'ws_down')}
    del _L0_ffn_all
    return {'x': x, 'ctx_2048': ctx_2048, 'L0_xattn_Wq': _L0_xattn_in['Wq'], 'L0_xattn_Wk': _L0_xattn_in['Wk'], 'L0_xattn_Wv': _L0_xattn_in['Wv'], 'L0_attn_W_qkv': _L0_attn_in['W_qkv'], 'L0_attn_b_qkv': _L0_attn_in['b_qkv'], 'L0_attn_W_out': _L0_attn_in['W_out'], 'L0_attn_b_out': _L0_attn_in['b_out'], 'L0_ffn_gate_w': _L0_ffn_in['gate_w'], 'L0_ffn_w_gate_up': _L0_ffn_in['w_gate_up'], 'L0_ffn_w_down': _L0_ffn_in['w_down'], 'L0_ffn_ws_gate_up': _L0_ffn_in['ws_gate_up'], 'L0_ffn_ws_down': _L0_ffn_in['ws_down']}

def reference(x, ctx_2048, L0_xattn_Wq, L0_xattn_Wk, L0_xattn_Wv, L0_attn_W_qkv, L0_attn_b_qkv, L0_attn_W_out, L0_attn_b_out, L0_ffn_gate_w, L0_ffn_w_gate_up, L0_ffn_w_down, L0_ffn_ws_gate_up, L0_ffn_ws_down):
    import jax
    import jax.numpy as jnp

    def _L0_xattn_ref(x, context, Wq, Wk, Wv):
        import jax, jax.numpy as jnp
        import numpy as np
        DIM = 256
        NHEADS = 32
        HEAD_DIM = DIM // NHEADS
        EPS = 1e-06

        def _rmsnorm(t):
            return t * jax.lax.rsqrt(jnp.mean(t * t, axis=-1, keepdims=True) + EPS)
        b, n, _ = x.shape
        m = context.shape[1]
        q = x @ Wq.T
        k_raw = context @ Wk.T
        v_raw = context @ Wv.T
        q = q.reshape(b, n, NHEADS, HEAD_DIM).transpose(0, 2, 1, 3)
        kv = jnp.concatenate([k_raw, v_raw], axis=-1)
        kv = kv.reshape(b, m, NHEADS, HEAD_DIM, 2)
        k = kv[..., 0].transpose(0, 2, 1, 3)
        v = kv[..., 1].transpose(0, 2, 1, 3)
        q = _rmsnorm(q)
        k = _rmsnorm(k)
        scale = HEAD_DIM ** (-0.5)
        scores = jnp.einsum('bhnd,bhmd->bhnm', q, k) * scale
        attn = jax.nn.softmax(scores, axis=-1)
        out = jnp.einsum('bhnm,bhmd->bhnd', attn, v)
        return out.transpose(0, 2, 1, 3).reshape(b, n, NHEADS * HEAD_DIM)

    def _L0_attn_ref(x, W_qkv, b_qkv, W_out, b_out):
        import jax, jax.numpy as jnp
        import numpy as np
        EMB = 256
        HEADS = 16
        B, S, E = x.shape
        H = HEADS
        dh = E // H
        qkv = x @ W_qkv + b_qkv
        qkv = qkv.reshape(B, S, H, 3 * dh).transpose(0, 2, 1, 3)
        q, k, v = jnp.split(qkv, 3, axis=-1)
        q = q / jnp.asarray(dh, q.dtype) ** 0.5
        scores = jnp.einsum('bhqd,bhkd->bhqk', q, k)
        weights = jax.nn.softmax(scores, axis=-1)
        attn = jnp.einsum('bhqk,bhkd->bhqd', weights, v)
        attn = attn.transpose(0, 2, 1, 3).reshape(B, S, E)
        return attn @ W_out + b_out

    def _L0_ffn_ref(hidden_states, gate_w, w_gate_up, w_down, ws_gate_up, ws_down):
        import jax, jax.numpy as jnp
        import numpy as np
        HIDDEN = 256
        FFN = 176
        N_EXPERTS = 64
        TOP_K = 6
        N_SHARED = 2
        SHARED_FFN = FFN * N_SHARED
        ROUTED_SCALING = 1.0
        EPS = 1e-20

        def _moe_forward(x, gate_w, w_gate_up, w_down, ws_gate_up, ws_down):
            T = x.shape[0]
            logits = jnp.einsum('th,eh->te', x.astype(jnp.float32), gate_w.astype(jnp.float32))
            scores = jax.nn.softmax(logits, axis=-1)
            topk_w, topk_ids = jax.lax.top_k(scores, TOP_K)
            topk_w = topk_w / (jnp.sum(topk_w, axis=-1, keepdims=True) + EPS)
            topk_w = topk_w * ROUTED_SCALING
            comb = jnp.zeros((T, N_EXPERTS), dtype=x.dtype)
            comb = comb.at[jnp.arange(T)[:, None], topk_ids].add(topk_w.astype(x.dtype))
            gu = jnp.einsum('th,efh->tef', x, w_gate_up)
            g, u = (gu[..., :FFN], gu[..., FFN:])
            act = jax.nn.silu(g) * u
            act = act * comb[:, :, None]
            routed = jnp.einsum('tef,ehf->th', act, w_down)
            sgu = jnp.einsum('th,fh->tf', x, ws_gate_up)
            sg, su = (sgu[..., :SHARED_FFN], sgu[..., SHARED_FFN:])
            shared = jnp.einsum('tf,hf->th', jax.nn.silu(sg) * su, ws_down)
            return routed + shared
        B, S, H = hidden_states.shape
        x = hidden_states.reshape(-1, H)
        out = _moe_forward(x, gate_w, w_gate_up, w_down, ws_gate_up, ws_down)
        return out.reshape(B, S, H)
    x = x + _L0_xattn_ref(_layernorm(x, axis=-1), ctx_2048, L0_xattn_Wq, L0_xattn_Wk, L0_xattn_Wv)
    x = x + _L0_attn_ref(_layernorm(x, axis=-1), L0_attn_W_qkv, L0_attn_b_qkv, L0_attn_W_out, L0_attn_b_out)
    x = x + _L0_ffn_ref(_layernorm(x, axis=-1), L0_ffn_gate_w, L0_ffn_w_gate_up, L0_ffn_w_down, L0_ffn_ws_gate_up, L0_ffn_ws_down)
    return x

_drawn_inputs = setup_inputs


def setup_inputs(seed=0):
    import zlib

    import numpy as np

    out = dict(_drawn_inputs(seed))
    spreads = {}
    factors = {'L0_attn_W_qkv': 2.924,
     'L0_attn_b_qkv': 8.0,
     'L0_attn_W_out': 2.696,
     'L0_attn_b_out': 2.956,
     'L0_ffn_gate_w': 7.936,
     'L0_ffn_w_gate_up': 6.595,
     'L0_ffn_w_down': 6.671,
     'L0_ffn_ws_gate_up': 2.882,
     'L0_ffn_ws_down': 2.871}
    for name, (base, spread) in spreads.items():
        noise = np.random.default_rng([zlib.crc32(name.encode()), seed]).standard_normal(out[name].shape)
        drawn = base * np.exp(spread * noise) if base else spread * noise
        out[name] = jnp.asarray(drawn.astype(out[name].dtype))
    for name, factor in factors.items():
        out[name] = (out[name] * factor).astype(out[name].dtype)
    return out
```

```python
from contextlib import ExitStack

import concourse.bass as bass
from concourse import mybir

P = 128
B = 2
D = 256
KT = D // P
TOK = B * P
CTX = 2048
XH, XD = 32, 8
NG = XH // 4
CHUNKS = B * CTX // P
GRP = 4
GROUPS = CHUNKS // GRP
CPB = CTX // P
PAIRS = CPB // 2
VW = XD + 1
SH, SD = 16, 16
SQ = SH // 4
SVW = SD + 1
E, FFN, TOPK = 64, 176, 6
ROUTED_TILES = E * FFN // P
SHARED_TILES = 3
TILES = ROUTED_TILES + SHARED_TILES
TILE_W = 2 * KT * P + D
SLOTS = 4
LN_EPS, RMS_EPS, TOPK_EPS = 1e-5, 1e-6, 1e-20
QK_UP = 64.0
COMB_UP = 1024.0
W_UP = 64.0
X_UP = 16.0
ACT_UP = 16.0
SEED = 0.68 * 2.0 ** -65

ALU = mybir.AluOpType
ACT = mybir.ActivationFunctionType
AX = mybir.AxisListType.X
F32 = mybir.dt.float32
F16 = mybir.dt.float16
U32 = mybir.dt.uint32


class Steps:

    def __init__(self, eng, sem):
        self.eng, self.sem, self.base, self.n = eng, sem, 0, 0

    def __call__(self, ins):
        ins.then_inc(self.sem, 1)
        self.n += 1

    def wait(self):
        self.eng.wait_ge(self.sem, self.base + self.n)

    def then(self, ins):
        self(ins)
        self.wait()

    def enter(self, i, per_turn):
        self.start, self.per, self.base, self.n = self.base + self.n, per_turn, self.base + self.n + i * per_turn, 0

    def leave(self, turns):
        assert self.n == self.per, (self.n, self.per)
        self.base, self.n = self.start + turns * self.per, 0


def perceiver(nc, x, ctxT, wq, wkv, wqk, wsv, bqk, bv, wout, bout, gate, moe, out):
    with ExitStack() as stack:
        def sb(name, shape, dt=F32):
            return stack.enter_context(nc.sbuf_tensor(name, shape, dt))

        def ps(name, shape, dt=F32):
            return stack.enter_context(nc.psum_tensor(name, shape, dt))

        def sem(name):
            return stack.enter_context(nc.semaphore(name))

        sc = [ps("scores0", [P, 1024]), ps("scores1", [P, 1024])]
        pj = [ps("proj0", [P, 512]), ps("proj1", [P, 512])]
        turn_bank = ps("turn", [P, 512])
        av = ps("av", [P, 512])

        ident = sb("ident", [P, P])
        ident_h = sb("ident_h", [P, P], F16)
        pick = sb("pick", [P, 2, 2, VW])
        ones_row = sb("ones_row", [1, P])
        wq_sb = sb("wq_sb", [P, KT, D])
        wkv_sb = sb("wkv_sb", [P, KT, 2 * D])
        wqk_sb = sb("wqk_sb", [P, KT, 2 * SQ, P])
        wsv_sb = sb("wsv_sb", [P, KT, D])
        bqk_sb = sb("bqk_sb", [P, 2 * SQ])
        bv_sb = sb("bv_sb", [1, D])
        wout_sb = sb("wout_sb", [P, KT, D])
        bout_sb = sb("bout_sb", [1, D])
        gate_sb = sb("gate_sb", [P, KT, E])
        xres = sb("xres", [P, B, D])
        h = sb("h", [P, B, D])
        hT = sb("hT", [P, KT, TOK])
        stats = sb("stats", [P, B, 6])
        mv = sb("mv", [P, B, 2])
        rs_x = sb("rs_x", [P, GRP * XH])
        rs_h = sb("rs_h", [P, GRP * XH])
        rs_t = sb("rs_t", [P, GRP * XH])
        rs_y = sb("rs_y", [P, GRP * XH])
        early = sb("early", [P, 9 * GRP * D + GRP * XH * 4 * XD // 2 * 2])

        def carve(space):
            taken = [0]

            def room(n):
                taken[0] += n
                assert taken[0] <= space.shape[1], (taken, space.shape)
                return space[:, taken[0] - n:taken[0]]
            return room

        room = carve(early[:, :])
        ctx_in_sb = room(2 * KT * GRP * P).rearrange("p (s k n) -> p s k n", s=2, k=KT)
        kraw = room(2 * GRP * D).rearrange("p (s n) -> p s n", s=2)
        ksq = room(2 * GRP * D).rearrange("p (s n) -> p s n", s=2)
        kn = room(GRP * D)
        k32 = room(GRP * XH * 4 * XD).bitcast(F16).rearrange("p (s h r) -> p s h r", s=2, h=GRP * XH)
        kT = sb("kT", [P, NG, B * CTX], F16)
        v_all = sb("v_all", [P, NG, CHUNKS, 4 * VW])
        qbd = sb("qbd", [P, NG, B, 4 * P], F16)
        room = carve(early[:, :])
        k_stage = room(CTX).bitcast(F16).rearrange("p (b n) -> p b n", b=B)
        v_stage = sb("v_stage", [P, 2, CPB, 4 * VW])
        q_stage = sb("q_stage", [P, 2, 4 * P], F16)
        probs = room(4 * 1024).rearrange("p (u n) -> p u n", u=4)
        av_all = room(2 * NG * 2 * P).rearrange("p (u n) -> p u n", u=2 * NG)

        room = carve(kT[:, :, :].rearrange("p g n -> p (g n)").bitcast(F32))
        qT = room(SQ * TOK).rearrange("p (s t) -> p s t", s=SQ)
        kTs = room(SQ * TOK).rearrange("p (s t) -> p s t", s=SQ)
        kbd = room(B * SQ * 512).rearrange("p (b s n) -> p b s n", b=B, s=SQ)
        sv = room(B * SH * SVW).rearrange("p (b h d) -> p b h d", b=B, h=SH)
        ssub = room(2 * 512).rearrange("p (u n) -> p u n", u=2)
        sprob = room(2 * 512).rearrange("p (u n) -> p u n", u=2)
        sprobT = room(2 * 512).rearrange("p (u n) -> p u n", u=2)
        vroom = v_all[:, :, :, :].rearrange("p g c n -> p (g c n)")
        ring = probs[:, :, :].rearrange("p u n -> p (u n)")[:, 0:SLOTS * TILE_W].rearrange("p (s n) -> p s n", s=SLOTS)
        onehot = vroom.bitcast(F16)[:, 0:E * FFN]
        smax = sb("smax", [P, 8])
        srec = sb("srec", [P, B, XH])
        ppad = sb("ppad", [P, B, E + 2])
        prep = sb("prep", [P, B, E + 2])
        top8 = sb("top8", [P, B, 8])
        topk = sb("topk", [P, B, 8])
        rstat = sb("rstat", [P, B, 4])
        comb = sb("comb", [P, B, E])
        comb_hl = sb("comb_hl", [P, B, 2, E], F16)
        combT = sb("combT", [P, TOK], F16)
        sil = room(2 * TOK).rearrange("p (u t) -> p u t", u=2)
        gated = room(2 * TOK).rearrange("p (u t) -> p u t", u=2)
        act_sb = room(2 * TOK).rearrange("p (u t) -> p u t", u=2)
        act_hl = room(SLOTS * TOK).bitcast(F16).rearrange("p (u two t) -> p u two t", u=SLOTS, two=2)
        xT_hl = room(KT * TOK).bitcast(F16).rearrange("p (two k t) -> p two k t", two=2, k=KT)
        w_hl = room(SLOTS * TILE_W).bitcast(F16).rearrange("p (s two n) -> p s two n", s=SLOTS, two=2)
        final = h

        x_in, wq_in, wkv_in, attn_in, y_out = (sem(n) for n in ("x_in", "wq_in", "wkv_in", "attn_in", "y_out"))
        ctx_in = [sem("ctx_in0"), sem("ctx_in1")]
        moe_in = [sem(f"moe_in{s}") for s in range(SLOTS)]
        half_in = sem("half_in")
        ident_zero, ident_done, onehot_step = sem("ident_zero"), sem("ident_done"), sem("onehot_step")
        dve_step = sem("dve_step")
        act_step = sem("act_step")
        h_ready, hT_turned, hT_ready = sem("h_ready"), sem("hT_turned"), sem("hT_ready")
        q_ready = sem("q_ready")
        kv_ready, kv_taken = sem("kv_ready"), sem("kv_taken")
        normed, turned, turn_free = sem("normed"), sem("turned"), sem("turn_free")
        staged, scores_ready, probs_ready = sem("staged"), sem("scores_ready"), sem("probs_ready")
        av_ready, av_taken, merged = sem("av_ready"), sem("av_taken"), sem("merged")
        qkv_ready, qT_ready, kT_plain, kbd_ready, sv_ready = (
            sem(n) for n in ("qkv_ready", "qT_ready", "kT_plain", "kbd_ready", "sv_ready"))
        s_ready, s_shifted, s_exp, p_turned, pT_ready, o_ready = (
            sem(n) for n in ("s_ready", "s_shifted", "s_exp", "p_turned", "pT_ready", "o_ready"))
        o_norm, oT_turned, oT_ready, y_ready = sem("o_norm"), sem("oT_turned"), sem("oT_ready"), sem("y_ready")
        logits_ready, logits_shifted, gate_exp = sem("logits_ready"), sem("logits_shifted"), sem("gate_exp")
        comb_ready, comb_turned, combT_ready = sem("comb_ready"), sem("comb_turned"), sem("combT_ready")
        xhi_ready, xlo_ready, whi_ready, wlo_ready = (sem(n) for n in ("xhi_ready", "xlo_ready", "whi_ready", "wlo_ready"))
        up_ready, sil_ready, weighed, ahi_ready, alo_ready, down_done = (
            sem(n) for n in ("up_ready", "sil_ready", "weighed", "ahi_ready", "alo_ready", "down_done"))
        final_ready = sem("final_ready")

        block = stack.enter_context(nc.Block())

        @block.sync
        def _(sp):
            sp.dma_start(xres[:, :, :], x).then_inc(x_in, 16)
            sp.dma_start(wq_sb[:, :, :], wq).then_inc(wq_in, 16)

            def load_ctx(slot, grp):
                sp.dma_start(ctx_in_sb[:, slot, :, :], ctxT[:, :, bass.ts(grp, GRP * P)]).then_inc(ctx_in[slot], 16)

            load_ctx(0, 0)
            sp.dma_start(wkv_sb[:, :, :], wkv).then_inc(wkv_in, 16)
            load_ctx(1, 1)
            for dst, src in ((wqk_sb[:, :, :, :], wqk), (wsv_sb[:, :, :], wsv), (bqk_sb[:, :], bqk), (bv_sb[:, :], bv),
                             (wout_sb[:, :, :], wout), (bout_sb[:, :], bout), (gate_sb[:, :, :], gate)):
                sp.dma_start(dst, src).then_inc(attn_in, 16)
            with sp.Fori(0, GROUPS // 2 - 1) as i:
                for slot in range(2):
                    sp.wait_ge(kv_ready, GRP * (2 * i + slot + 1))
                    load_ctx(slot, 2 * i + 2 + slot)

            def load_tile(slot, t):
                sp.dma_start(ring[:, slot, :], moe[t, :, :]).then_inc(moe_in[slot], 16)

            sp.wait_ge(av_ready, 2 * NG)
            for t in range(SLOTS):
                load_tile(t, t)
            sp.wait_ge(onehot_step, 3)
            sp.dma_start(onehot[E:P, :], onehot[0:E, :]).then_inc(half_in, 16)
            with sp.Fori(0, TILES // SLOTS - 1) as i:
                for slot in range(SLOTS):
                    sp.wait_ge(wlo_ready, SLOTS * i + slot + 1)
                    load_tile(slot, SLOTS * i + SLOTS + slot)
            for t in range(TILES // SLOTS * SLOTS, TILES):
                sp.wait_ge(wlo_ready, t - SLOTS + 1)
                load_tile(t % SLOTS, t)
            sp.wait_ge(final_ready, 1)
            sp.dma_start(out, final[:, :, :]).then_inc(y_out, 16)
            sp.wait_ge(y_out, 16)

        @block.gpsimd
        def _(pool):
            nc.gpsimd.memset(ident[:, :], 0.0).then_inc(ident_zero, 1)
            pool.wait_ge(ident_zero, 1)
            nc.gpsimd.affine_select(out=ident[:, :], in_=ident[:, :], compare_op=ALU.not_equal, fill=1.0, base=0,
                                    pattern=[[-1, P]], channel_multiplier=1).then_inc(ident_done, 1)
            nc.gpsimd.memset(qbd[:, :, :, :], 0.0).then_inc(ident_done, 1)
            nc.gpsimd.memset(v_all[:, :, :, :].rearrange("p g c (h d) -> p (g c h) d", d=VW)[:, :, XD:VW],
                             1.0).then_inc(ident_done, 1)
            pool.wait_ge(av_taken, 2 * NG)
            nc.gpsimd.memset(onehot[0:E, :], 1.0).then_inc(onehot_step, 1)
            pool.wait_ge(onehot_step, 1)
            nc.gpsimd.affine_select(out=onehot[0:E, :], in_=onehot[0:E, :], compare_op=ALU.is_ge, fill=0.0, base=0,
                                    pattern=[[1, E * FFN]], channel_multiplier=-FFN).then_inc(onehot_step, 1)
            pool.wait_ge(onehot_step, 2)
            nc.gpsimd.affine_select(out=onehot[0:E, :], in_=onehot[0:E, :], compare_op=ALU.is_ge, fill=0.0,
                                    base=FFN - 1, pattern=[[-1, E * FFN]],
                                    channel_multiplier=FFN).then_inc(onehot_step, 1)

        @block.tensor
        def _(pe):
            def turn_h(n, src, ready, turned):
                pe.wait_ge(ready, n)
                for kt in range(KT):
                    for b in range(B):
                        last = nc.tensor.transpose(pj[0][:, (kt * B + b) * P:(kt * B + b + 1) * P],
                                                   src[:, b, kt * P:(kt + 1) * P], ident[:, :])
                last.then_inc(turned, 1)

            def rows(bank, b, w, width, bias=None, at=None):
                o = bank[:, at:at + width]
                if bias is not None:
                    nc.tensor.matmul(o, ones_row[:, :], bias, start=True, stop=False)
                for kt in range(KT):
                    last = nc.tensor.matmul(o, hT[:, kt, b * P:(b + 1) * P], w[:, kt, :],
                                            start=(kt == 0 and bias is None), stop=(kt == KT - 1))
                return last

            pe.wait_ge(ident_done, 1)
            turn_h(1, h, h_ready, hT_turned)
            pe.wait_ge(hT_ready, 1)
            pe.wait_ge(wq_in, 16)
            for b in range(B):
                last = rows(pj[1], b, wq_sb, D, at=b * D)
            last.then_inc(q_ready, 1)
            pe.wait_ge(normed, 1)
            for b in range(B):
                dst = (turn_bank, av)[b][:, :].bitcast(F16)
                for g in range(NG):
                    src = k32[:, 0, b * XH + 4 * g:b * XH + 4 * g + 4, :].rearrange("p h r -> p (h r)")
                    last = nc.tensor.transpose(dst[:, g * P:(g + 1) * P], src, ident_h[:, :])
                last.then_inc(turned, 1)

            def project(slot, grp, loads):
                pe.wait_ge(ctx_in[slot], loads)
                for c in range(GRP):
                    if not (isinstance(grp, int) and grp == 0 and c < 2):
                        pe.wait_ge(kv_taken, grp * GRP + c - 1)
                    for kt in range(KT):
                        last = nc.tensor.matmul(pj[c % 2][:, :], ctx_in_sb[:, slot, kt, c * P:(c + 1) * P],
                                                wkv_sb[:, kt, :], start=(kt == 0), stop=(kt == KT - 1))
                    last.then_inc(kv_ready, 1)

            def turn_keys(slot, grp):
                pe.wait_ge(normed, grp + 2)
                for c in range(GRP):
                    pe.wait_ge(turn_free, grp * GRP + c + 1)
                    dst = (turn_bank, av)[c % 2][:, :].bitcast(F16)
                    for g in range(NG):
                        src = k32[:, slot, c * XH + 4 * g:c * XH + 4 * g + 4, :].rearrange("p h r -> p (h r)")
                        last = nc.tensor.transpose(dst[:, g * P:(g + 1) * P], src, ident_h[:, :])
                    last.then_inc(turned, 1)

            pe.wait_ge(wkv_in, 16)
            project(0, 0, 16)
            with pe.Fori(0, GROUPS // 2 - 1) as i:
                project(1, 2 * i + 1, 16 * i + 16)
                turn_keys(0, 2 * i)
                project(0, 2 * i + 2, 16 * i + 32)
                turn_keys(1, 2 * i + 1)
            project(1, GROUPS - 1, 16 * GROUPS // 2)
            turn_keys(0, GROUPS - 2)
            turn_keys(1, GROUPS - 1)

            def scores(k):
                b, cp = k // PAIRS % 2, k % PAIRS
                for half in range(2):
                    c = 2 * cp + half
                    last = nc.tensor.matmul(sc[k % 2][:, half * 512:(half + 1) * 512],
                                            k_stage[:, b, c * P:(c + 1) * P], q_stage[:, b, :], start=True, stop=True)
                last.then_inc(scores_ready, 1)

            def weigh(k):
                b, cp = k // PAIRS, k % PAIRS
                for two in range(2):
                    for half in range(2):
                        j = 2 * two + half
                        last = nc.tensor.matmul(
                            (turn_bank, av)[b][32 * j:32 * j + 2 * VW, 0:2 * P],
                            v_stage[:, b, 2 * cp + half, two * 2 * VW:(two + 1) * 2 * VW],
                            probs[:, k % 4, half * 512 + two * 256:half * 512 + (two + 1) * 256],
                            start=(cp == 0), stop=(cp == PAIRS - 1), tile_position=(0, 32 * j), skip_group_check=True)
                if cp == PAIRS - 1:
                    last.then_inc(av_ready, 1)

            def quad(g, more):
                for k in range(2 * PAIRS):
                    pe.wait_ge(probs_ready, 2 * PAIRS * g + k + 1)
                    if k + 2 < 2 * PAIRS or more:
                        if k + 2 == PAIRS:
                            pe.wait_ge(staged, 2 * g + 2)
                        if k + 2 == 2 * PAIRS:
                            pe.wait_ge(staged, 2 * g + 3)
                        scores(k + 2)
                    weigh(k)

            pe.wait_ge(kv_taken, CHUNKS)
            pe.wait_ge(staged, 1)
            scores(0)
            scores(1)
            with pe.Fori(0, NG - 1) as g:
                quad(g, True)
            quad(NG - 1, False)
            for b in range(B):
                for g in range(NG):
                    n = 2 * g + b
                    pe.wait_ge(av_taken, n + 1)
                    for ab in range(2):
                        last = nc.tensor.matmul(pj[b][:, (2 * g + ab) * 2 * VW:(2 * g + ab + 1) * 2 * VW],
                                                av_all[:, n, ab * P:(ab + 1) * P],
                                                pick[:, ab, :, :].rearrange("p t d -> p (t d)"),
                                                start=True, stop=True)
                last.then_inc(merged, 1)

            turn_h(2, h, h_ready, hT_turned)
            pe.wait_ge(hT_ready, 2)
            pe.wait_ge(attn_in, 7 * 16)
            for s in range(2 * SQ):
                for kt in range(KT):
                    last = nc.tensor.matmul(sc[s // 4][:, s % 4 * TOK:(s % 4 + 1) * TOK], wqk_sb[:, kt, s, :],
                                            hT[:, kt, :], start=(kt == 0), stop=(kt == KT - 1))
            last.then_inc(qkv_ready, 1)
            for b in range(B):
                last = rows(pj[1], b, wsv_sb, D, bias=bv_sb[:, :], at=b * D)
            last.then_inc(qkv_ready, 1)

            def self_scores(u):
                b, s = u // SQ, u % SQ
                if u >= 4:
                    pe.wait_ge(s_shifted, u - 3)
                nc.tensor.matmul(sc[u // 2 % 2][:, u % 2 * 512:(u % 2 + 1) * 512], qT[:, s, b * P:(b + 1) * P],
                                 kbd[:, b, s, :], start=True, stop=True).then_inc(s_ready, 1)

            def self_turn(u):
                pe.wait_ge(s_exp, u + 1)
                if u >= 1:
                    pe.wait_ge(pT_ready, u)
                for j in range(4):
                    last = nc.tensor.transpose(pj[0][:, j * P:(j + 1) * P], sprob[:, u % 2, j * P:(j + 1) * P],
                                               ident[:, :])
                last.then_inc(p_turned, 1)

            def self_weigh(u):
                b, s = u // SQ, u % SQ
                pe.wait_ge(pT_ready, u + 1)
                for j in range(4):
                    head = 4 * s + j
                    last = nc.tensor.matmul((turn_bank, av)[b][:, head * SVW:(head + 1) * SVW],
                                            sprobT[:, u % 2, j * P:(j + 1) * P], sv[:, b, head, :],
                                            start=True, stop=True)
                last.then_inc(o_ready, 1)

            units = B * SQ
            pe.wait_ge(qT_ready, 1)
            pe.wait_ge(kbd_ready, 1)
            for u in range(2):
                self_scores(u)
            pe.wait_ge(sv_ready, 1)
            for u in range(units):
                if u + 2 < units:
                    self_scores(u + 2)
                self_turn(u)
                if u >= 1:
                    self_weigh(u - 1)
            self_weigh(units - 1)
            turn_h(1, h, o_norm, oT_turned)
            pe.wait_ge(oT_ready, 1)
            for b in range(B):
                last = rows(pj[1], b, wout_sb, D, bias=bout_sb[:, :], at=b * D)
            last.then_inc(y_ready, 1)

            turn_h(3, h, h_ready, hT_turned)
            pe.wait_ge(hT_ready, 3)
            for b in range(B):
                last = rows(turn_bank, b, gate_sb, E, at=b * E)
            last.then_inc(logits_ready, 1)
            pe.wait_ge(comb_ready, 1)
            for b in range(B):
                last = nc.tensor.transpose(av[:, :].bitcast(F16)[:, b * P:(b + 1) * P],
                                           comb_hl[:, b, :, :].rearrange("p t e -> p (t e)"), ident_h[:, :])
            last.then_inc(comb_turned, 1)

            HALVES = ((0, 0), (0, 1), (1, 0))

            def up(s, t, routed=True):
                slot = s % SLOTS
                pe.wait_ge(wlo_ready, t + 1)
                bank = sc[slot // 2][:, slot % 2 * 512:(slot % 2 + 1) * 512]
                for gu in range(2):
                    for kt in range(KT):
                        at = (gu * KT + kt) * P
                        for n, (wh, xh) in enumerate(HALVES):
                            last = nc.tensor.matmul(bank[:, gu * TOK:(gu + 1) * TOK], w_hl[:, slot, wh, at:at + P],
                                                    xT_hl[:, xh, kt, :], start=(kt == 0 and n == 0),
                                                    stop=(kt == KT - 1 and n == len(HALVES) - 1))
                if routed:
                    if not (isinstance(t, int) and t < 2):
                        pe.wait_ge(weighed, t - 1)
                    last = nc.tensor.matmul((turn_bank, av)[s % 2][:, 0:TOK], onehot[:, bass.ts(t, P)],
                                            combT[:, :], start=True, stop=True)
                last.then_inc(up_ready, 1)

            def down(s, t):
                slot = s % SLOTS
                pe.wait_ge(alo_ready, t + 1)
                for b in range(B):
                    for n, (ah, wh) in enumerate(HALVES):
                        last = nc.tensor.matmul(pj[b][:, 0:D], act_hl[:, slot, ah, b * P:(b + 1) * P],
                                                w_hl[:, slot, wh, 2 * KT * P:TILE_W],
                                                start=(isinstance(t, int) and t == 0 and n == 0),
                                                stop=(isinstance(t, int) and t == TILES - 1 and n == len(HALVES) - 1),
                                                skip_group_check=True)
                last.then_inc(down_done, 1)

            pe.wait_ge(xlo_ready, 1)
            pe.wait_ge(combT_ready, 1)
            pe.wait_ge(half_in, 16)
            pe.wait_ge(onehot_step, 3)
            up(0, 0)
            up(1, 1)
            up(2, 2)
            down(0, 0)
            up(3, 3)
            down(1, 1)
            with pe.Fori(0, ROUTED_TILES // SLOTS - 1) as i:
                for s in range(SLOTS):
                    up(s, SLOTS * i + SLOTS + s)
                    down(s - 2, SLOTS * i + SLOTS + s - 2)
            for t in range(ROUTED_TILES, TILES):
                up(t, t, False)
                down(t - 2, t - 2)
            down(TILES - 2, TILES - 2)
            down(TILES - 1, TILES - 1)

        @block.scalar
        def _(act):
            def take_kv(slot, grp):
                for c in range(GRP):
                    act.wait_ge(kv_ready, grp * GRP + c + 1)
                    if c == 0 and not (isinstance(grp, int) and grp == 0):
                        act.wait_ge(normed, grp)
                    src = pj[c % 2]
                    nc.scalar.activation(ksq[:, slot, c * D:(c + 1) * D], src[:, 0:D], ACT.Square)
                    nc.scalar.activation(kraw[:, slot, c * D:(c + 1) * D], src[:, 0:D], ACT.Copy)
                    dst = v_all[:, :, bass.ds(grp * GRP + c, 1), :].rearrange(
                        "p g c (h d) -> p g (c h) d", h=4)[:, :, :, 0:XD]
                    nc.scalar.activation(dst, src[:, D:2 * D].rearrange("p (g h d) -> p g h d", g=NG, h=4),
                                         ACT.Copy).then_inc(kv_taken, 1)

            def take_keys(grp):
                for c in range(GRP):
                    act.wait_ge(turned, B + grp * GRP + c + 1)
                    src = (turn_bank, av)[c % 2][:, :].bitcast(F16).rearrange("p (g n) -> p g n", g=NG)
                    nc.scalar.activation(kT[:, :, bass.ts(grp * GRP + c, P)], src, ACT.Copy).then_inc(turn_free, 1)

            act.wait_ge(ident_done, 3)
            take_kv(0, 0)
            with act.Fori(0, GROUPS // 2 - 1) as i:
                take_kv(1, 2 * i + 1)
                take_keys(2 * i)
                take_kv(0, 2 * i + 2)
                take_keys(2 * i + 1)
            take_kv(1, GROUPS - 1)
            take_keys(GROUPS - 2)
            take_keys(GROUPS - 1)

            with act.Fori(0, NG) as g:
                for k in range(2 * PAIRS):
                    act.wait_ge(scores_ready, 2 * PAIRS * g + k + 1)
                    nc.scalar.activation(probs[:, k % 4, :], sc[k % 2][:, :], ACT.Exp,
                                         scale=XD ** -0.5 / QK_UP ** 2).then_inc(probs_ready, 1)

            act.wait_ge(qkv_ready, 1)
            for s in range(SQ):
                last = nc.scalar.activation(kTs[:, s, :], sc[1][:, s * TOK:(s + 1) * TOK], ACT.Identity,
                                            bias=bqk_sb[:, SQ + s:SQ + s + 1])
            last.then_inc(kT_plain, 1)
            units = B * SQ
            for u in range(units + 1):
                if u < units:
                    act.wait_ge(s_shifted, u + 1)
                    if u >= 2:
                        act.wait_ge(p_turned, u - 1)
                    nc.scalar.activation(sprob[:, u % 2, :], ssub[:, u % 2, :], ACT.Exp).then_inc(s_exp, 1)
                if u >= 1:
                    act.wait_ge(p_turned, u)
                    if u >= 3:
                        act.wait_ge(o_ready, u - 2)
                    nc.scalar.activation(sprobT[:, (u - 1) % 2, :], pj[0][:, :], ACT.Copy).then_inc(pT_ready, 1)

            for b in range(B):
                act.wait_ge(logits_shifted, b + 1)
                nc.scalar.activation(comb[:, b, :], comb[:, b, :], ACT.Exp,
                                     accum_out=rstat[:, b, 1:2]).then_inc(gate_exp, 1)

            act.wait_ge(hT_ready, 3)
            nc.scalar.activation(xT_hl[:, 0, :, :], hT[:, :, :], ACT.Copy, scale=X_UP).then_inc(xhi_ready, 1)

            def split_hi(s, t, loads):
                slot = s % SLOTS
                act.wait_ge(moe_in[slot], loads)
                if not (isinstance(t, int) and t < SLOTS):
                    act.wait_ge(down_done, t - SLOTS + 1)
                nc.scalar.activation(w_hl[:, slot, 0, :], ring[:, slot, :], ACT.Copy, scale=W_UP).then_inc(whi_ready, 1)

            def silu(s, t):
                act.wait_ge(up_ready, t + 1)
                if not (isinstance(t, int) and t < 2):
                    act.wait_ge(weighed, t - 1)
                slot = s % SLOTS
                nc.scalar.activation(sil[:, s % 2, :], sc[slot // 2][:, slot % 2 * 512:slot % 2 * 512 + TOK],
                                     ACT.Silu, scale=1.0 / (W_UP * X_UP)).then_inc(sil_ready, 1)

            def split_act_hi(s, t):
                act.wait_ge(weighed, t + 1)
                nc.scalar.activation(act_hl[:, s % SLOTS, 0, :], act_sb[:, s % 2, :], ACT.Copy).then_inc(ahi_ready, 1)

            split_hi(0, 0, 16)
            split_hi(1, 1, 16)
            for t in range(2):
                silu(t, t)
                split_hi(t + 2, t + 2, 16)
                split_act_hi(t, t)
            with act.Fori(0, ROUTED_TILES // SLOTS - 1) as i:
                for s in range(2, 2 + SLOTS):
                    silu(s, SLOTS * i + s)
                    split_hi(s + 2, SLOTS * i + s + 2, 16 * i + 16 * (1 + (s + 2) // SLOTS))
                    split_act_hi(s, SLOTS * i + s)
            for t in range(ROUTED_TILES - 2, TILES):
                silu(t, t)
                if t + 2 < TILES:
                    split_hi(t + 2, t + 2, 16 * (1 + (t + 2) // SLOTS))
                split_act_hi(t, t)

        @block.vector
        def _(dve):
            step = Steps(dve, dve_step)
            v = nc.vector

            def rsqrt(n):
                x_, h_, t_, y_ = (a[:, 0:n] for a in (rs_x, rs_h, rs_t, rs_y))
                step(v.tensor_scalar(h_, x_, -0.5, None, ALU.mult))
                step.then(v.tensor_scalar(t_.bitcast(U32), x_.bitcast(U32), 1, 0x7FFFFFFF,
                                          ALU.logical_shift_right, ALU.bitwise_xor))
                step.then(v.tensor_scalar(y_, t_, SEED, None, ALU.mult))
                for _ in range(3):
                    step.then(v.tensor_tensor(t_, y_, y_, ALU.mult))
                    step.then(v.tensor_tensor(t_, t_, h_, ALU.mult))
                    step.then(v.scalar_tensor_tensor(out=y_, in0=t_, scalar=1.5, in1=y_, op0=ALU.add, op1=ALU.mult))

            def layernorm():
                for b in range(B):
                    step(v.bn_stats(stats[:, b, :], xres[:, b, :]))
                step.wait()
                for b in range(B):
                    step(v.bn_aggr(mv[:, b, :], stats[:, b, :]))
                step.wait()
                step.then(v.tensor_scalar(rs_x[:, 0:B], mv[:, :, 1], LN_EPS, None, ALU.add))
                rsqrt(B)
                for b in range(B):
                    last = v.tensor_scalar(h[:, b, :], xres[:, b, :], mv[:, b, 0:1], rs_y[:, b:b + 1],
                                           ALU.subtract, ALU.mult)
                last.then_inc(h_ready, 1)

            def take_hT(n, turned, ready):
                dve.wait_ge(turned, n)
                v.tensor_copy(hT[:, :, :].rearrange("p k t -> p (k t)"), pj[0][:, :]).then_inc(ready, 1)

            def normalise(raw, sq, hi_lo, heads, lo_at):
                step.then(v.tensor_reduce(rs_t[:, 0:heads], sq.rearrange("p (h d) -> p h d", d=XD), AX, ALU.add))
                step.then(v.tensor_scalar(rs_x[:, 0:heads], rs_t[:, 0:heads], 1.0 / XD, RMS_EPS, ALU.mult, ALU.add))
                rsqrt(heads)
                n3 = kn[:, 0:heads * XD].rearrange("p (h d) -> p h d", d=XD)
                step.then(v.scalar_tensor_tensor(out=n3, in0=raw.rearrange("p (h d) -> p h d", d=XD), scalar=QK_UP,
                                                 in1=rs_y[:, 0:heads].unsqueeze(2).broadcast_to([P, heads, XD]),
                                                 op0=ALU.mult, op1=ALU.mult))
                step.then(v.tensor_copy(hi_lo[:, :, 0:XD], n3))
                step.then(v.tensor_tensor(hi_lo[:, :, lo_at:lo_at + XD], n3, hi_lo[:, :, 0:XD], ALU.subtract))

            step(v.memset(ones_row[:, :], 1.0))
            dve.wait_ge(ident_done, 1)
            step(v.tensor_copy(ident_h[:, :], ident[:, :]))
            idv = ident[:, :].rearrange("p (t half n) -> p t half n", t=2, half=2)
            for ab in range(2):
                step(v.tensor_tensor(pick[:, ab, :, :], idv[:, :, 0, ab * VW:(ab + 1) * VW],
                                     idv[:, :, 1, ab * VW:(ab + 1) * VW], ALU.add))

            dve.wait_ge(x_in, 16)
            layernorm()
            take_hT(1, hT_turned, hT_ready)
            dve.wait_ge(q_ready, 1)
            step.then(v.tensor_copy(kraw[:, 1, 0:B * D], pj[1][:, :]))
            step.then(v.tensor_tensor(ksq[:, 1, 0:B * D], kraw[:, 1, 0:B * D], kraw[:, 1, 0:B * D], ALU.mult))
            q32 = k32[:, 0, 0:B * XH, :]
            normalise(kraw[:, 1, 0:B * D], ksq[:, 1, 0:B * D], q32, B * XH, 2 * XD)
            q_halves = q32.rearrange("p h (half two d) -> p h half two d", half=2, two=2)
            v.tensor_copy(q_halves[:, :, :, 1, :], q_halves[:, :, :, 0, :]).then_inc(normed, 1)
            dve.wait_ge(ident_done, 2)
            for b in range(B):
                dve.wait_ge(turned, b + 1)
                src = (turn_bank, av)[b][:, :].bitcast(F16).rearrange("p (g n) -> p g n", g=NG)
                for j in range(4):
                    last = v.tensor_copy(qbd[32 * j:32 * j + 32, :, b, j * P:(j + 1) * P], src[32 * j:32 * j + 32, :, :])
                last.then_inc(turn_free, 1)

            def normalise_keys(slot, grp):
                dve.wait_ge(kv_taken, GRP * grp + GRP)
                if not (isinstance(grp, int) and grp == 0):
                    dve.wait_ge(turned, B + GRP * grp - GRP)
                normalise(kraw[:, slot, :], ksq[:, slot, :], k32[:, slot, :, :], GRP * XH, XD)
                v.tensor_copy(k32[:, slot, :, 2 * XD:], k32[:, slot, :, 0:2 * XD]).then_inc(normed, 1)

            normalise_keys(0, 0)
            with dve.Fori(0, GROUPS // 2 - 1) as i:
                step.enter(i, 2 * 17)
                normalise_keys(1, 2 * i + 1)
                normalise_keys(0, 2 * i + 2)
            step.leave(GROUPS // 2 - 1)
            normalise_keys(1, GROUPS - 1)

            def stage(b, g):
                v.tensor_copy(k_stage[:, b, :], kT[:, bass.ds(g, 1), b * CTX:(b + 1) * CTX].rearrange(
                    "p g n -> p (g n)"))
                v.tensor_copy(v_stage[:, b, :, :].rearrange("p c n -> p (c n)"),
                              v_all[:, bass.ds(g, 1), b * CPB:(b + 1) * CPB, :].rearrange("p g c n -> p (g c n)"))
                v.tensor_copy(q_stage[:, b, :], qbd[:, bass.ds(g, 1), b, :].rearrange(
                    "p g n -> p (g n)")).then_inc(staged, 1)

            def take_av(b, g):
                dve.wait_ge(av_ready, 2 * g + b + 1)
                v.tensor_copy(av_all[:, bass.ds(2 * g + b, 1), :].rearrange("p u n -> p (u n)"),
                              (turn_bank, av)[b][:, 0:2 * P]).then_inc(av_taken, 1)

            dve.wait_ge(turn_free, B + CHUNKS)
            for b in range(B):
                step.then(v.memset((turn_bank, av)[b][:, :], 0.0))
            stage(0, 0)
            stage(1, 0)
            with dve.Fori(0, NG - 1) as g:
                for b in range(B):
                    take_av(b, g)
                    stage(b, g + 1)
            for b in range(B):
                take_av(b, NG - 1)
            for b in range(B):
                dve.wait_ge(merged, b + 1)
                got = pj[b][:, 0:XH * VW].rearrange("p (g ab t d) -> p g t ab d", g=NG, ab=2, t=2)
                rec = srec[:, b, :].rearrange("p (g t ab) -> p g t ab", g=NG, t=2)
                step.then(v.reciprocal(rec, got[:, :, :, :, XD]))
                new = h[:, b, :].rearrange("p (g t ab d) -> p g t ab d", g=NG, t=2, ab=2)
                for ab in range(2):
                    step(v.tensor_tensor(new[:, :, :, ab, :], got[:, :, :, ab, 0:XD],
                                         rec[:, :, :, ab].unsqueeze(3).broadcast_to([P, NG, 2, XD]), ALU.mult))
                step.wait()
                step.then(v.tensor_tensor(xres[:, b, :], xres[:, b, :], h[:, b, :], ALU.add))

            layernorm()
            take_hT(2, hT_turned, hT_ready)
            step(v.memset(kbd, 0.0))
            step(v.memset(sv[:, :, :, SD:SVW], 1.0))
            step.wait()
            dve.wait_ge(qkv_ready, 1)
            for s in range(SQ):
                last = v.tensor_scalar(qT[:, s, :], sc[0][:, s * TOK:(s + 1) * TOK], bqk_sb[:, s:s + 1], SD ** -0.5,
                                       ALU.add, ALU.mult)
            last.then_inc(qT_ready, 1)
            dve.wait_ge(kT_plain, 1)
            for j in range(4):
                rows_ = slice(32 * j, 32 * j + 32)
                last = v.tensor_copy(kbd[rows_, :, :, j * P:(j + 1) * P],
                                     kTs[rows_, :, :].rearrange("p s (b n) -> p b s n", b=B))
            last.then_inc(kbd_ready, 1)
            dve.wait_ge(qkv_ready, 2)
            v.tensor_copy(sv[:, :, :, 0:SD], pj[1][:, :].rearrange("p (b h d) -> p b h d", b=B, h=SH)).then_inc(sv_ready, 1)
            for u in range(B * SQ):
                dve.wait_ge(s_ready, u + 1)
                src = sc[u // 2 % 2][:, u % 2 * 512:(u % 2 + 1) * 512].rearrange("p (h n) -> p h n", h=4)
                top = smax[:, u % 2 * 4:u % 2 * 4 + 4]
                step.then(v.tensor_reduce(top, src, AX, ALU.max))
                if u >= 2:
                    dve.wait_ge(s_exp, u - 1)
                v.tensor_tensor(ssub[:, u % 2, :].rearrange("p (h n) -> p h n", h=4), src,
                                top.unsqueeze(2).broadcast_to([P, 4, P]), ALU.subtract).then_inc(s_shifted, 1)
            for b in range(B):
                dve.wait_ge(o_ready, SQ * (b + 1))
                got = (turn_bank, av)[b][:, 0:SH * SVW].rearrange("p (h d) -> p h d", d=SVW)
                step.then(v.reciprocal(srec[:, b, 0:SH], got[:, :, SD]))
                last = v.tensor_tensor(h[:, b, :].rearrange("p (h d) -> p h d", d=SD), got[:, :, 0:SD],
                                       srec[:, b, 0:SH].unsqueeze(2).broadcast_to([P, SH, SD]), ALU.mult)
            last.then_inc(o_norm, 1)
            take_hT(1, oT_turned, oT_ready)
            dve.wait_ge(y_ready, 1)
            xflat = xres[:, :, :].rearrange("p b n -> p (b n)")
            step.then(v.tensor_tensor(xflat, xflat, pj[1][:, :], ALU.add))

            layernorm()
            take_hT(3, hT_turned, hT_ready)
            step(v.memset(ppad[:, :, E:E + 1], -1.0))
            step(v.memset(ppad[:, :, E + 1:E + 2], -2.0))
            step(v.memset(topk[:, :, TOPK:TOPK + 1], -1.0))
            step(v.memset(topk[:, :, TOPK + 1:TOPK + 2], -2.0))
            dve.wait_ge(logits_ready, 1)
            for b in range(B):
                lg = turn_bank[:, b * E:(b + 1) * E]
                step.then(v.tensor_reduce(rstat[:, b, 0:1], lg, AX, ALU.max))
                v.tensor_scalar(comb[:, b, :], lg, rstat[:, b, 0:1], None, ALU.subtract).then_inc(logits_shifted, 1)
            for b in range(B):
                dve.wait_ge(gate_exp, b + 1)
                step.then(v.reciprocal(rstat[:, b, 2:3], rstat[:, b, 1:2]))
                step.then(v.tensor_scalar(ppad[:, b, 0:E], comb[:, b, :], rstat[:, b, 2:3], None, ALU.mult))
                step.then(v.max(top8[:, b, :], ppad[:, b, :]))
                step.then(v.tensor_copy(topk[:, b, 0:TOPK], top8[:, b, 0:TOPK]))
                step(v.match_replace(out=prep[:, b, :], in_to_replace=topk[:, b, :], in_values=ppad[:, b, :],
                                     imm_value=-3.0))
                step.then(v.tensor_reduce(rstat[:, b, 0:1], topk[:, b, 0:TOPK], AX, ALU.add))
                step.then(v.tensor_scalar(rstat[:, b, 3:4], rstat[:, b, 0:1], TOPK_EPS, None, ALU.add))
                step.then(v.reciprocal(rstat[:, b, 0:1], rstat[:, b, 3:4]))
                step.then(v.tensor_tensor(prep[:, b, 0:E], ppad[:, b, 0:E], prep[:, b, 0:E], ALU.not_equal))
                step.then(v.scalar_tensor_tensor(out=comb[:, b, :], in0=ppad[:, b, 0:E], scalar=rstat[:, b, 0:1],
                                                 in1=prep[:, b, 0:E], op0=ALU.mult, op1=ALU.mult))
                step.then(v.tensor_scalar(comb[:, b, :], comb[:, b, :], COMB_UP, None, ALU.mult))
                step.then(v.tensor_copy(comb_hl[:, b, 0, :], comb[:, b, :]))
                step(v.tensor_tensor(comb_hl[:, b, 1, :], comb[:, b, :], comb_hl[:, b, 0, :], ALU.subtract))
            step.wait()
            v.nop().then_inc(comb_ready, 1)
            dve.wait_ge(comb_turned, 1)
            v.tensor_copy(combT[:, :], av[:, :].bitcast(F16)[:, 0:TOK]).then_inc(combT_ready, 1)

            dve.wait_ge(xhi_ready, 1)
            v.scalar_tensor_tensor(out=xT_hl[:, 1, :, :].rearrange("p k t -> p (k t)"),
                                   in0=hT[:, :, :].rearrange("p k t -> p (k t)"), scalar=X_UP,
                                   in1=xT_hl[:, 0, :, :].rearrange("p k t -> p (k t)"),
                                   op0=ALU.mult, op1=ALU.subtract).then_inc(xlo_ready, 1)

            def split_lo(s, t):
                slot = s % SLOTS
                dve.wait_ge(whi_ready, t + 1)
                v.scalar_tensor_tensor(out=w_hl[:, slot, 1, :], in0=ring[:, slot, :], scalar=W_UP,
                                       in1=w_hl[:, slot, 0, :], op0=ALU.mult, op1=ALU.subtract).then_inc(wlo_ready, 1)

            def gate_up(s, t, routed=True):
                slot = s % SLOTS
                upv = sc[slot // 2][:, slot % 2 * 512 + TOK:(slot % 2 + 1) * 512]
                dve.wait_ge(sil_ready, t + 1)
                share = COMB_UP if routed else 1.0
                to = gated if routed else act_sb
                first = v.scalar_tensor_tensor(out=to[:, s % 2, :], in0=upv, scalar=ACT_UP / (W_UP * X_UP * share),
                                               in1=sil[:, s % 2, :], op0=ALU.mult, op1=ALU.mult)
                if routed:
                    step.then(first)
                    v.tensor_tensor(act_sb[:, s % 2, :], gated[:, s % 2, :], (turn_bank, av)[s % 2][:, 0:TOK],
                                    ALU.mult).then_inc(weighed, 1)
                else:
                    first.then_inc(weighed, 1)

            def split_act_lo(s, t):
                slot = s % SLOTS
                dve.wait_ge(ahi_ready, t + 1)
                v.tensor_tensor(act_hl[:, slot, 1, :], act_sb[:, s % 2, :], act_hl[:, slot, 0, :],
                                ALU.subtract).then_inc(alo_ready, 1)

            split_lo(0, 0)
            split_lo(1, 1)
            for t in range(2):
                gate_up(t, t)
                split_lo(t + 2, t + 2)
                split_act_lo(t, t)
            with dve.Fori(0, ROUTED_TILES // SLOTS - 1) as i:
                step.enter(i, SLOTS)
                for s in range(2, 2 + SLOTS):
                    gate_up(s, SLOTS * i + s)
                    split_lo(s + 2, SLOTS * i + s + 2)
                    split_act_lo(s, SLOTS * i + s)
            step.leave(ROUTED_TILES // SLOTS - 1)
            for t in range(ROUTED_TILES - 2, TILES):
                gate_up(t, t, t < ROUTED_TILES)
                if t + 2 < TILES:
                    split_lo(t + 2, t + 2)
                split_act_lo(t, t)
            dve.wait_ge(down_done, TILES)
            for b in range(B):
                last = v.scalar_tensor_tensor(out=final[:, b, :], in0=pj[b][:, 0:D], scalar=1.0 / (W_UP * ACT_UP),
                                              in1=xres[:, b, :], op0=ALU.mult, op1=ALU.add)
            last.then_inc(final_ready, 1)


def kernel(**inputs):
    import numpy as np
    import concourse.bacc as bacc
    from concourse.bass_utils import run_bass_kernel_spmd

    a = {k: np.asarray(v) for k, v in inputs.items()}

    def kparts(w):
        return np.ascontiguousarray(w.reshape(KT, P, -1).transpose(1, 0, 2))

    arrays = {"x": np.ascontiguousarray(a["x"].transpose(1, 0, 2))}
    arrays["ctxT"] = kparts(a["ctx_2048"].reshape(B * CTX, D).T)
    arrays["wq"] = kparts(a["L0_xattn_Wq"].T)
    w = np.concatenate([a["L0_xattn_Wk"], a["L0_xattn_Wv"]]).reshape(D, 2, D)
    arrays["wkv"] = kparts(np.concatenate([w[:, 0].T, w[:, 1].T], axis=1))
    wqkv = a["L0_attn_W_qkv"].reshape(D, SH, 3, SD)
    bqkv = a["L0_attn_b_qkv"].reshape(SH, 3, SD)
    wide = np.zeros((D, 2, SH, 32), wqkv.dtype)
    wide[..., :SD] = wqkv[:, :, :2].transpose(0, 2, 1, 3)
    arrays["wqk"] = kparts(wide.reshape(D, -1)).reshape(P, KT, 2 * SQ, P)
    wide = np.zeros((2, SH, 32), bqkv.dtype)
    wide[..., :SD] = bqkv[:, :2].transpose(1, 0, 2)
    arrays["bqk"] = np.ascontiguousarray(wide.reshape(2 * SQ, P).T)
    arrays["wsv"] = kparts(wqkv[:, :, 2].reshape(D, D))
    arrays["bv"] = np.ascontiguousarray(bqkv[:, 2].reshape(1, D))
    arrays["wout"] = kparts(a["L0_attn_W_out"])
    arrays["bout"] = a["L0_attn_b_out"].reshape(1, D)
    arrays["gate"] = kparts(a["L0_ffn_gate_w"].T)
    gu, dn = a["L0_ffn_w_gate_up"], a["L0_ffn_w_down"]
    sgu, sdn = a["L0_ffn_ws_gate_up"], a["L0_ffn_ws_down"]
    moe = np.zeros((TILES, P, TILE_W), gu.dtype)
    for n, (routed, shared) in enumerate(((gu[:, :FFN], sgu[:2 * FFN]), (gu[:, FFN:], sgu[2 * FFN:]))):
        rows = np.zeros((TILES * P, D), gu.dtype)
        rows[:E * FFN] = routed.reshape(-1, D)
        rows[E * FFN:E * FFN + 2 * FFN] = shared
        moe[:, :, n * KT * P:(n + 1) * KT * P] = rows.reshape(TILES, P, KT, P).transpose(0, 3, 2, 1).reshape(
            TILES, P, KT * P)
    rows = np.zeros((TILES * P, D), gu.dtype)
    rows[:E * FFN] = dn.transpose(0, 2, 1).reshape(-1, D)
    rows[E * FFN:E * FFN + 2 * FFN] = sdn.T
    moe[:, :, 2 * KT * P:] = rows.reshape(TILES, P, D)
    arrays["moe"] = moe

    nc = bacc.Bacc("TRN2", target_bir_lowering=False, num_devices=1)
    order = ["x", "ctxT", "wq", "wkv", "wqk", "wsv", "bqk", "bv", "wout", "bout", "gate", "moe"]
    args = [nc.dram_tensor(f"{n}_dram", arrays[n].shape, F32, kind="ExternalInput").ap() for n in order]
    out = nc.dram_tensor("out_dram", (P, B, D), F32, kind="ExternalOutput").ap()
    perceiver(nc, *args, out)
    r = run_bass_kernel_spmd(nc, [{f"{n}_dram": arrays[n] for n in order}], core_ids=[0])
    return np.ascontiguousarray(r.results[0]["out_dram"].transpose(1, 0, 2))
```

```python
from contextlib import ExitStack

import concourse.bass as bass
from concourse import mybir

P = 128
B = 2
D = 256
KT = D // P
TOK = B * P
CTX = 2048
XH, XD = 32, 8
NG = XH // 4
CHUNKS = B * CTX // P
GRP = 4
GROUPS = CHUNKS // GRP
CPB = CTX // P
PAIRS = CPB // 2
VW = XD + 1
SH, SD = 16, 16
SQ = SH // 4
SVW = SD + 1
E, FFN, TOPK = 64, 176, 6
ROUTED_TILES = E * FFN // P
SHARED_TILES = 3
TILES = ROUTED_TILES + SHARED_TILES
TILE_W = 2 * KT * P + D
SLOTS = 4
LN_EPS, RMS_EPS, TOPK_EPS = 1e-5, 1e-6, 1e-20
QK_UP = 64.0
KBD_DVE = 5
AV_DOWN = 2.0 ** -6
COMB_UP = 1024.0
W_UP = 64.0
X_UP = 16.0
ACT_UP = 16.0
CTX_UP = 16.0
WKV_UP = 64.0
SEED = 0.68 * 2.0 ** -65

ALU = mybir.AluOpType
ACT = mybir.ActivationFunctionType
AX = mybir.AxisListType.X
F32 = mybir.dt.float32
F16 = mybir.dt.float16
U32 = mybir.dt.uint32


class Steps:

    def __init__(self, eng, sem):
        self.eng, self.sem, self.base, self.n = eng, sem, 0, 0

    def __call__(self, ins):
        ins.then_inc(self.sem, 1)
        self.n += 1

    def wait(self):
        self.eng.wait_ge(self.sem, self.base + self.n)

    def then(self, ins):
        self(ins)
        self.wait()

    def enter(self, i, first, per_turn):
        self.start, self.per = self.base + self.n, per_turn
        self.base, self.n = self.start - first * per_turn + i * per_turn, 0

    def leave(self, turns):
        assert self.n == self.per, (self.n, self.per)
        self.base, self.n = self.start + turns * self.per, 0


def perceiver(nc, x, ctxT, wq, wkv, wqk, wsv, bqk, bv, wout, bout, gate, moe, out):
    with ExitStack() as stack:
        def sb(name, shape, dt=F32):
            return stack.enter_context(nc.sbuf_tensor(name, shape, dt))

        def ps(name, shape, dt=F32):
            return stack.enter_context(nc.psum_tensor(name, shape, dt))

        def sem(name):
            return stack.enter_context(nc.semaphore(name))

        sc = [ps("scores0", [P, 1024]), ps("scores1", [P, 1024])]
        pj = [ps("proj0", [P, 512]), ps("proj1", [P, 512])]
        turn_bank = ps("turn", [P, 512])
        av = ps("av", [P, 512])

        ident = sb("ident", [P, P])
        ident_h = sb("ident_h", [P, P], F16)
        pick = sb("pick", [P, 2, 2, VW], F16)
        ones_row = sb("ones_row", [1, P])
        wq_sb = sb("wq_sb", [P, KT, D])
        wkv_sb = sb("wkv_sb", [P, KT, 2 * D])
        wkv_hl = sb("wkv_hl", [P, 2, KT, 2 * D], F16)
        wqk_sb = sb("wqk_sb", [P, KT, 2 * KT, P])
        wsv_sb = sb("wsv_sb", [P, KT, D])
        bqk_sb = sb("bqk_sb", [P, 2 * KT])
        own_rows = sb("own_rows", [P, P // SD])
        bv_sb = sb("bv_sb", [1, D])
        wout_sb = sb("wout_sb", [P, KT, D])
        bout_sb = sb("bout_sb", [1, D])
        gate_sb = sb("gate_sb", [P, KT, E])
        xres = sb("xres", [P, B, D])
        h = sb("h", [P, B, D])
        hT = sb("hT", [P, KT, TOK])
        stats = sb("stats", [P, B, 6])
        mv = sb("mv", [P, B, 2])
        rs_x = sb("rs_x", [P, GRP * XH])
        rs_h = sb("rs_h", [P, GRP * XH])
        rs_t = sb("rs_t", [P, GRP * XH])
        rs_y = sb("rs_y", [P, GRP * XH])
        early = sb("early", [P, 9 * GRP * D + GRP * XH * 4 * XD // 2 * 2])

        def carve(space):
            taken = [0]

            def room(n):
                taken[0] += n
                assert taken[0] <= space.shape[1], (taken, space.shape)
                return space[:, taken[0] - n:taken[0]]
            return room

        HALVES = ((0, 0), (0, 1), (1, 0))

        room = carve(early[:, :])
        ctx_in_sb = room(2 * KT * GRP * P).rearrange("p (s k n) -> p s k n", s=2, k=KT)
        kraw = room(2 * GRP * D).rearrange("p (s n) -> p s n", s=2)
        ksq = room(2 * GRP * D).rearrange("p (s n) -> p s n", s=2)
        kn = room(GRP * D)
        k32 = room(GRP * XH * 4 * XD).bitcast(F16).rearrange("p (s h r) -> p s h r", s=2, h=GRP * XH)
        ctx_hl = room(2 * KT * GRP * P).bitcast(F16).rearrange("p (s two n) -> p s two n", s=2, two=2)
        kT = sb("kT", [P, NG, B * CTX], F16)
        v_all = sb("v_all", [P, NG, CHUNKS, 4 * VW])
        qbd = sb("qbd", [P, NG, B, 4 * P], F16)
        room = carve(early[:, :])
        k_stage = room(CTX).bitcast(F16).rearrange("p (b n) -> p b n", b=B)
        v_stage = sb("v_stage", [P, 2, CPB, 4 * VW])
        q_stage = sb("q_stage", [P, 2, 4 * P], F16)
        q_sq = q_stage[:, :, :].rearrange("p b n -> p (b n)").bitcast(F32)
        q32 = v_stage[:, :, :, :].rearrange("p b c n -> p (b c n)").bitcast(F16)[:, 0:B * XH * 4 * XD].rearrange(
            "p (h r) -> p h r", h=B * XH)
        q_raw = h[:, :, :].rearrange("p b n -> p (b n)")
        probs = room(4 * 1024).rearrange("p (u n) -> p u n", u=4)
        av_hl = room(2 * NG * 2 * P).bitcast(F16).rearrange("p (u two n) -> p u two n", u=2 * NG, two=2)

        room = carve(kT[:, :, :].rearrange("p g n -> p (g n)").bitcast(F32))
        qT = room(KT * TOK).rearrange("p (k t) -> p k t", k=KT)
        kTs = room(KT * TOK).rearrange("p (k t) -> p k t", k=KT)
        kbd = room(B * SH * P).rearrange("p (b k j n) -> p b k j n", b=B, k=KT, j=P // SD)
        sv = room(B * SH * SVW).rearrange("p (b h d) -> p b h d", b=B, h=SH)
        ssub = room(2 * 512).rearrange("p (u n) -> p u n", u=2)
        sprob = room(2 * 512).rearrange("p (u n) -> p u n", u=2)
        sprobT = room(2 * 512).rearrange("p (u n) -> p u n", u=2)
        vroom = v_all[:, :, :, :].rearrange("p g c n -> p (g c n)")
        ring = probs[:, :, :].rearrange("p u n -> p (u n)")[:, 0:SLOTS * TILE_W].rearrange("p (s n) -> p s n", s=SLOTS)
        onehot = vroom.bitcast(F16)[:, 0:E * FFN]
        smax = sb("smax", [P, 8])
        srec = sb("srec", [P, B, XH])
        ppad = sb("ppad", [P, B, E + 2])
        prep = sb("prep", [P, B, E + 2])
        top8 = sb("top8", [P, B, 8])
        topk = sb("topk", [P, B, 8])
        rstat = sb("rstat", [P, 4, B])
        comb = sb("comb", [P, B, E])
        comb_hl = sb("comb_hl", [P, B, 2, E], F16)
        combT = sb("combT", [P, TOK], F16)
        sil = room(2 * TOK).rearrange("p (u t) -> p u t", u=2)
        gated = room(2 * TOK).rearrange("p (u t) -> p u t", u=2)
        act_sb = room(2 * TOK).rearrange("p (u t) -> p u t", u=2)
        act_hl = room(SLOTS * TOK).bitcast(F16).rearrange("p (u two t) -> p u two t", u=SLOTS, two=2)
        xT_hl = room(KT * TOK).bitcast(F16).rearrange("p (two k t) -> p two k t", two=2, k=KT)
        w_hl = room(SLOTS * TILE_W).bitcast(F16).rearrange("p (s two n) -> p s two n", s=SLOTS, two=2)
        final = h

        x_in, wq_in, wkv_in, attn_in, y_out = (sem(n) for n in ("x_in", "wq_in", "wkv_in", "attn_in", "y_out"))
        ctx_in = [sem("ctx_in0"), sem("ctx_in1")]
        moe_in = [sem(f"moe_in{s}") for s in range(SLOTS)]
        half_in = sem("half_in")
        ident_zero, ident_done, onehot_step = sem("ident_zero"), sem("ident_done"), sem("onehot_step")
        dve_step = sem("dve_step")
        act_step = sem("act_step")
        h_ready, hT_turned, hT_ready = sem("h_ready"), sem("hT_turned"), sem("hT_ready")
        q_ready, q_normed, q_turned, q_taken = (sem(n) for n in ("q_ready", "q_normed", "q_turned", "q_taken"))
        kv_ready, kv_taken = sem("kv_ready"), sem("kv_taken")
        wkv_hi, wkv_lo, ctx_lo = (sem(n) for n in ("wkv_hi", "wkv_lo", "ctx_lo"))
        sums_ready, roots_ready = sem("sums_ready"), sem("roots_ready")
        normed, turned, turn_free = sem("normed"), sem("turned"), sem("turn_free")
        staged, scores_ready, probs_ready = sem("staged"), sem("scores_ready"), sem("probs_ready")
        av_ready, av_taken, merged = sem("av_ready"), sem("av_taken"), sem("merged")
        qkv_ready, qT_ready, kT_plain, kbd_ready, sv_ready = (
            sem(n) for n in ("qkv_ready", "qT_ready", "kT_plain", "kbd_ready", "sv_ready"))
        s_ready, s_shifted, s_exp, p_turned, pT_ready, o_ready = (
            sem(n) for n in ("s_ready", "s_shifted", "s_exp", "p_turned", "pT_ready", "o_ready"))
        o_norm, oT_turned, oT_ready, y_ready = sem("o_norm"), sem("oT_turned"), sem("oT_ready"), sem("y_ready")
        logits_ready, logits_shifted, gate_exp, own_done = (
            sem(n) for n in ("logits_ready", "logits_shifted", "gate_exp", "own_done"))
        comb_ready, comb_turned, combT_ready = sem("comb_ready"), sem("comb_turned"), sem("combT_ready")
        xhi_ready, xlo_ready, whi_ready, wlo_ready = (sem(n) for n in ("xhi_ready", "xlo_ready", "whi_ready", "wlo_ready"))
        up_ready, sil_ready, weighed, ahi_ready, alo_ready, down_done = (
            sem(n) for n in ("up_ready", "sil_ready", "weighed", "ahi_ready", "alo_ready", "down_done"))
        final_ready = sem("final_ready")

        block = stack.enter_context(nc.Block())

        @block.sync
        def _(sp):
            def load_ctx(slot, grp):
                sp.dma_start(ctx_in_sb[:, slot, :, :], ctxT[:, :, bass.ts(grp, GRP * P)]).then_inc(ctx_in[slot], 16)

            sp.dma_start(xres[:, :, :], x).then_inc(x_in, 16)
            sp.dma_start(wkv_sb[:, :, :], wkv).then_inc(wkv_in, 16)
            load_ctx(0, 0)
            sp.dma_start(wq_sb[:, :, :], wq).then_inc(wq_in, 16)
            load_ctx(1, 1)
            for dst, src in ((wqk_sb[:, :, :, :], wqk), (wsv_sb[:, :, :], wsv), (bqk_sb[:, :], bqk), (bv_sb[:, :], bv),
                             (wout_sb[:, :, :], wout), (bout_sb[:, :], bout), (gate_sb[:, :, :], gate)):
                sp.dma_start(dst, src).then_inc(attn_in, 16)
            with sp.Fori(0, GROUPS // 2 - 1) as i:
                for slot in range(2):
                    sp.wait_ge(ctx_lo, 2 * i + slot + 1)
                    load_ctx(slot, 2 * i + 2 + slot)

            def load_tile(slot, t):
                sp.dma_start(ring[:, slot, :], moe[t, :, :]).then_inc(moe_in[slot], 16)

            sp.wait_ge(av_ready, 2 * NG)
            for t in range(SLOTS):
                load_tile(t, t)
            sp.wait_ge(onehot_step, 3)
            sp.dma_start(onehot[E:P, :], onehot[0:E, :]).then_inc(half_in, 16)
            with sp.Fori(0, TILES // SLOTS - 1) as i:
                for slot in range(SLOTS):
                    sp.wait_ge(wlo_ready, SLOTS * i + slot + 1)
                    load_tile(slot, SLOTS * i + SLOTS + slot)
            for t in range(TILES // SLOTS * SLOTS, TILES):
                sp.wait_ge(wlo_ready, t - SLOTS + 1)
                load_tile(t % SLOTS, t)
            sp.wait_ge(final_ready, 1)
            sp.dma_start(out, final[:, :, :]).then_inc(y_out, 16)
            sp.wait_ge(y_out, 16)

        @block.gpsimd
        def _(pool):
            nc.gpsimd.memset(ident[:, :], 0.0).then_inc(ident_zero, 1)
            pool.wait_ge(ident_zero, 1)
            nc.gpsimd.affine_select(out=ident[:, :], in_=ident[:, :], compare_op=ALU.not_equal, fill=1.0, base=0,
                                    pattern=[[-1, P]], channel_multiplier=1).then_inc(ident_done, 1)
            nc.gpsimd.memset(qbd[:, :, :, :], 0.0).then_inc(ident_done, 1)
            nc.gpsimd.memset(v_all[:, :, :, :].rearrange("p g c (h d) -> p (g c h) d", d=VW)[:, :, XD:VW],
                             1.0).then_inc(ident_done, 1)
            nc.gpsimd.memset(own_rows[:, :], 1.0).then_inc(own_done, 1)
            pool.wait_ge(own_done, 1)
            nc.gpsimd.affine_select(out=own_rows[:, :], in_=own_rows[:, :], compare_op=ALU.is_ge, fill=0.0, base=0,
                                    pattern=[[-SD, P // SD]], channel_multiplier=1).then_inc(own_done, 1)
            pool.wait_ge(own_done, 2)
            nc.gpsimd.affine_select(out=own_rows[:, :], in_=own_rows[:, :], compare_op=ALU.is_ge, fill=0.0,
                                    base=SD - 1, pattern=[[SD, P // SD]], channel_multiplier=-1).then_inc(own_done, 1)
            pool.wait_ge(av_taken, 2 * NG)
            nc.gpsimd.memset(onehot[0:E, :], 1.0).then_inc(onehot_step, 1)
            pool.wait_ge(onehot_step, 1)
            nc.gpsimd.affine_select(out=onehot[0:E, :], in_=onehot[0:E, :], compare_op=ALU.is_ge, fill=0.0, base=0,
                                    pattern=[[1, E * FFN]], channel_multiplier=-FFN).then_inc(onehot_step, 1)
            pool.wait_ge(onehot_step, 2)
            nc.gpsimd.affine_select(out=onehot[0:E, :], in_=onehot[0:E, :], compare_op=ALU.is_ge, fill=0.0,
                                    base=FFN - 1, pattern=[[-1, E * FFN]],
                                    channel_multiplier=FFN).then_inc(onehot_step, 1)

        @block.tensor
        def _(pe):
            def turn_h(n, src, ready, turned):
                pe.wait_ge(ready, n)
                for kt in range(KT):
                    for b in range(B):
                        last = nc.tensor.transpose(sc[0][:, (kt * B + b) * P:(kt * B + b + 1) * P],
                                                   src[:, b, kt * P:(kt + 1) * P], ident[:, :])
                last.then_inc(turned, 1)

            def rows(bank, b, w, width, bias=None, at=None):
                o = bank[:, at:at + width]
                if bias is not None:
                    nc.tensor.matmul(o, ones_row[:, :], bias, start=True, stop=False)
                for kt in range(KT):
                    last = nc.tensor.matmul(o, hT[:, kt, b * P:(b + 1) * P], w[:, kt, :],
                                            start=(kt == 0 and bias is None), stop=(kt == KT - 1))
                return last

            def project(slot, grp, c):
                if c == 0:
                    pe.wait_ge(ctx_lo, grp + 1)
                if not (isinstance(grp, int) and grp == 0 and c < 2):
                    pe.wait_ge(kv_taken, grp * GRP + c - 1)
                for kt in range(KT):
                    for n, (ch, wh) in enumerate(HALVES):
                        at = kt * GRP * P + c * P
                        last = nc.tensor.matmul(pj[c % 2][:, :], ctx_hl[:, slot, ch, at:at + P], wkv_hl[:, wh, kt, :],
                                                start=(kt == 0 and n == 0), stop=(kt == KT - 1 and n == 2))
                last.then_inc(kv_ready, 1)

            def turn_keys(slot, grp, c):
                if c == 0:
                    pe.wait_ge(normed, grp + 1)
                if isinstance(grp, int) and grp == 0 and c < 2:
                    pe.wait_ge(q_taken, c + 1)
                else:
                    pe.wait_ge(turn_free, grp * GRP + c - 1)
                dst = (turn_bank, av)[c % 2][:, :].bitcast(F16)
                for g in range(NG):
                    src = k32[:, slot, c * XH + 4 * g:c * XH + 4 * g + 4, :].rearrange("p h r -> p (h r)")
                    last = nc.tensor.transpose(dst[:, g * P:(g + 1) * P], src, ident_h[:, :])
                last.then_inc(turned, 1)

            pe.wait_ge(wkv_lo, 1)
            for c in range(GRP):
                project(0, 0, c)
            pe.wait_ge(ident_done, 1)
            turn_h(1, h, h_ready, hT_turned)
            pe.wait_ge(hT_ready, 1)
            pe.wait_ge(wq_in, 16)
            for b in range(B):
                last = rows(sc[1], b, wq_sb, D, at=b * D)
            last.then_inc(q_ready, 1)
            for c in range(GRP):
                project(1, 1, c)
            pe.wait_ge(q_normed, 1)
            for b in range(B):
                dst = (turn_bank, av)[b][:, :].bitcast(F16)
                for g in range(NG):
                    src = q32[:, b * XH + 4 * g:b * XH + 4 * g + 4, :].rearrange("p h r -> p (h r)")
                    last = nc.tensor.transpose(dst[:, g * P:(g + 1) * P], src, ident_h[:, :])
                last.then_inc(q_turned, 1)

            def project_and_turn(i):
                for slot in range(2):
                    for c in range(GRP):
                        project(slot, 2 * i + slot, c)
                        turn_keys(slot, 2 * i + slot - 2, c)

            project_and_turn(1)
            with pe.Fori(2, GROUPS // 2) as i:
                project_and_turn(i)
            for slot in range(2):
                for c in range(GRP):
                    turn_keys(slot, GROUPS - 2 + slot, c)

            def scores(k):
                b, cp = k // PAIRS % 2, k % PAIRS
                for half in range(2):
                    c = 2 * cp + half
                    last = nc.tensor.matmul(sc[k % 2][:, half * 512:(half + 1) * 512],
                                            k_stage[:, b, c * P:(c + 1) * P], q_stage[:, b, :], start=True, stop=True)
                last.then_inc(scores_ready, 1)

            def weigh(k):
                b, cp = k // PAIRS, k % PAIRS
                for two in range(2):
                    for half in range(2):
                        j = 2 * two + half
                        last = nc.tensor.matmul(
                            pj[b][32 * j:32 * j + 2 * VW, 0:2 * P],
                            v_stage[:, b, 2 * cp + half, two * 2 * VW:(two + 1) * 2 * VW],
                            probs[:, k % 4, half * 512 + two * 256:half * 512 + (two + 1) * 256],
                            start=(cp == 0), stop=(cp == PAIRS - 1), tile_position=(0, 32 * j), skip_group_check=True)
                if cp == PAIRS - 1:
                    last.then_inc(av_ready, 1)

            def quad(g, more):
                for k in range(2 * PAIRS):
                    pe.wait_ge(probs_ready, 2 * PAIRS * g + k + 1)
                    if k + 2 < 2 * PAIRS or more:
                        if k + 2 == PAIRS:
                            pe.wait_ge(staged, 2 * g + 2)
                        if k + 2 == 2 * PAIRS:
                            pe.wait_ge(staged, 2 * g + 3)
                        scores(k + 2)
                    weigh(k)

            pe.wait_ge(kv_taken, CHUNKS)
            pe.wait_ge(staged, 1)
            scores(0)
            scores(1)
            with pe.Fori(0, NG - 1) as g:
                quad(g, True)
            quad(NG - 1, False)
            for b in range(B):
                for g in range(NG):
                    n = 2 * g + b
                    pe.wait_ge(av_taken, n + 1)
                    for ab in range(2):
                        for half in range(2):
                            last = nc.tensor.matmul((turn_bank, av)[b][:, (2 * g + ab) * 2 * VW:(2 * g + ab + 1) * 2 * VW],
                                                    av_hl[:, n, half, ab * P:(ab + 1) * P],
                                                    pick[:, ab, :, :].rearrange("p t d -> p (t d)"),
                                                    start=(half == 0), stop=(half == 1))
                last.then_inc(merged, 1)

            turn_h(2, h, h_ready, hT_turned)
            pe.wait_ge(hT_ready, 2)
            pe.wait_ge(attn_in, 7 * 16)
            for qk in (1, 0):
                for half in range(KT):
                    for kt in range(KT):
                        last = nc.tensor.matmul(sc[1][:, qk * 512 + half * TOK:qk * 512 + (half + 1) * TOK],
                                                wqk_sb[:, kt, KT * qk + half, :], hT[:, kt, :],
                                                start=(kt == 0), stop=(kt == KT - 1))
                last.then_inc(qkv_ready, 1)
            for b in range(B):
                last = rows(pj[0], b, wsv_sb, D, bias=bv_sb[:, :], at=b * D)
            last.then_inc(qkv_ready, 1)

            def self_scores(u):
                b, s = u // SQ, u % SQ
                if u >= 4:
                    pe.wait_ge(s_shifted, u - 3)
                nc.tensor.matmul(sc[u // 2 % 2][:, u % 2 * 512:(u % 2 + 1) * 512],
                                 qT[:, s // 2, b * P:(b + 1) * P],
                                 kbd[:, b, s // 2, s % 2 * 4:s % 2 * 4 + 4, :].rearrange("p j n -> p (j n)"),
                                 start=True, stop=True).then_inc(s_ready, 1)

            def self_turn(u):
                pe.wait_ge(s_exp, u + 1)
                if u >= 2:
                    pe.wait_ge(pT_ready, u - 1)
                for j in range(4):
                    last = nc.tensor.transpose(pj[u % 2][:, j * P:(j + 1) * P], sprob[:, u % 2, j * P:(j + 1) * P],
                                               ident[:, :])
                last.then_inc(p_turned, 1)

            def self_weigh(u):
                b, s = u // SQ, u % SQ
                pe.wait_ge(pT_ready, u + 1)
                for j in range(4):
                    head = 4 * s + j
                    last = nc.tensor.matmul((turn_bank, av)[b][:, head * SVW:(head + 1) * SVW],
                                            sprobT[:, u % 2, j * P:(j + 1) * P], sv[:, b, head, :],
                                            start=True, stop=True)
                last.then_inc(o_ready, 1)

            units = B * SQ
            pe.wait_ge(qT_ready, 1)
            pe.wait_ge(kbd_ready, 2)
            for u in range(2):
                self_scores(u)
            pe.wait_ge(sv_ready, 1)
            for u in range(units):
                if u + 2 < units:
                    self_scores(u + 2)
                self_turn(u)
                if u >= 1:
                    self_weigh(u - 1)
            self_weigh(units - 1)
            turn_h(1, h, o_norm, oT_turned)
            pe.wait_ge(oT_ready, 1)
            for b in range(B):
                last = rows(pj[1], b, wout_sb, D, bias=bout_sb[:, :], at=b * D)
            last.then_inc(y_ready, 1)

            turn_h(3, h, h_ready, hT_turned)
            pe.wait_ge(hT_ready, 3)
            for b in range(B):
                last = rows(turn_bank, b, gate_sb, E, at=b * E)
            last.then_inc(logits_ready, 1)

            def up(s, t, routed=True):
                slot = s % SLOTS
                pe.wait_ge(wlo_ready, t + 1)
                bank = sc[slot // 2][:, slot % 2 * 512:(slot % 2 + 1) * 512]
                for gu in range(2):
                    for kt in range(KT):
                        at = (gu * KT + kt) * P
                        for n, (wh, xh) in enumerate(HALVES):
                            last = nc.tensor.matmul(bank[:, gu * TOK:(gu + 1) * TOK], w_hl[:, slot, wh, at:at + P],
                                                    xT_hl[:, xh, kt, :], start=(kt == 0 and n == 0),
                                                    stop=(kt == KT - 1 and n == len(HALVES) - 1))
                if routed:
                    if not (isinstance(t, int) and t < 2):
                        pe.wait_ge(weighed, t - 1)
                    last = nc.tensor.matmul((turn_bank, av)[s % 2][:, 0:TOK], onehot[:, bass.ts(t - SHARED_TILES, P)],
                                            combT[:, :], start=True, stop=True)
                last.then_inc(up_ready, 1)

            def down(s, t):
                slot = s % SLOTS
                pe.wait_ge(alo_ready, t + 1)
                for b in range(B):
                    for n, (ah, wh) in enumerate(HALVES):
                        last = nc.tensor.matmul(pj[b][:, 0:D], act_hl[:, slot, ah, b * P:(b + 1) * P],
                                                w_hl[:, slot, wh, 2 * KT * P:TILE_W],
                                                start=(isinstance(t, int) and t == 0 and n == 0),
                                                stop=(isinstance(t, int) and t == TILES - 1 and n == len(HALVES) - 1),
                                                skip_group_check=True)
                last.then_inc(down_done, 1)

            pe.wait_ge(xlo_ready, 1)
            for t in range(SHARED_TILES):
                up(t, t, False)
            pe.wait_ge(comb_ready, 1)
            for b in range(B):
                last = nc.tensor.transpose(av[:, :].bitcast(F16)[:, b * P:(b + 1) * P],
                                           comb_hl[:, b, :, :].rearrange("p t e -> p (t e)"), ident_h[:, :])
            last.then_inc(comb_turned, 1)
            pe.wait_ge(combT_ready, 1)
            pe.wait_ge(half_in, 16)
            pe.wait_ge(onehot_step, 3)
            down(0, 0)
            up(3, 3)
            down(1, 1)
            with pe.Fori(0, TILES // SLOTS - 1) as i:
                for s in range(SLOTS):
                    up(s, SLOTS * i + SLOTS + s)
                    down(s - 2, SLOTS * i + SLOTS + s - 2)
            for t in range(TILES // SLOTS * SLOTS, TILES):
                up(t, t)
                down(t - 2, t - 2)
            down(TILES - 2, TILES - 2)
            down(TILES - 1, TILES - 1)

        @block.scalar
        def _(act):
            def take_kv(slot, grp, c):
                act.wait_ge(kv_ready, grp * GRP + c + 1)
                if c == 0 and not (isinstance(grp, int) and grp < 2):
                    act.wait_ge(normed, grp - 1)
                src, down = pj[c % 2], 1.0 / (CTX_UP * WKV_UP)
                nc.scalar.activation(ksq[:, slot, c * D:(c + 1) * D], src[:, 0:D], ACT.Square, scale=down)
                nc.scalar.activation(kraw[:, slot, c * D:(c + 1) * D], src[:, 0:D], ACT.Copy, scale=down)
                dst = v_all[:, :, bass.ds(grp * GRP + c, 1), :].rearrange(
                    "p g c (h d) -> p g (c h) d", h=4)[:, :, :, 0:XD]
                nc.scalar.activation(dst, src[:, D:2 * D].rearrange("p (g h d) -> p g h d", g=NG, h=4),
                                     ACT.Copy, scale=down).then_inc(kv_taken, 1)

            def take_keys(grp, c):
                act.wait_ge(turned, grp * GRP + c + 1)
                src = (turn_bank, av)[c % 2][:, :].bitcast(F16).rearrange("p (g n) -> p g n", g=NG)
                nc.scalar.activation(kT[:, :, bass.ts(grp * GRP + c, P)], src, ACT.Copy).then_inc(turn_free, 1)

            def roots(nth, n):
                act.wait_ge(sums_ready, nth)
                nc.scalar.activation(rs_x[:, 0:n], rs_t[:, 0:n], ACT.Sqrt).then_inc(roots_ready, 1)

            act.wait_ge(wkv_in, 16)
            nc.scalar.activation(wkv_hl[:, 0, :, :], wkv_sb[:, :, :], ACT.Copy, scale=WKV_UP).then_inc(wkv_hi, 1)
            roots(1, B)
            act.wait_ge(ident_done, 3)
            for c in range(GRP):
                take_kv(0, 0, c)
            roots(2, B * XH)
            for c in range(GRP):
                take_kv(1, 1, c)
                if c == 0:
                    roots(3, GRP * XH)

            def take_both(i):
                for slot in range(2):
                    for c in range(GRP):
                        take_kv(slot, 2 * i + slot, c)
                        take_keys(2 * i + slot - 2, c)
                        if c == 0:
                            roots(2 * i + slot + 2, GRP * XH)

            take_both(1)
            with act.Fori(2, GROUPS // 2) as i:
                take_both(i)
            for c in range(GRP):
                take_keys(GROUPS - 2, c)
                if c == 0:
                    roots(GROUPS + 2, GRP * XH)
            for c in range(GRP):
                take_keys(GROUPS - 1, c)

            with act.Fori(0, NG) as g:
                for k in range(2 * PAIRS):
                    act.wait_ge(scores_ready, 2 * PAIRS * g + k + 1)
                    nc.scalar.activation(probs[:, k % 4, :], sc[k % 2][:, :], ACT.Exp,
                                         scale=XD ** -0.5 / QK_UP ** 2).then_inc(probs_ready, 1)

            def split_hi(s, t, loads):
                slot = s % SLOTS
                act.wait_ge(moe_in[slot], loads)
                if not (isinstance(t, int) and t < SLOTS):
                    act.wait_ge(down_done, t - SLOTS + 1)
                nc.scalar.activation(w_hl[:, slot, 0, :], ring[:, slot, :], ACT.Copy, scale=W_UP).then_inc(whi_ready, 1)

            act.wait_ge(av_taken, 2 * NG)
            for t in range(SHARED_TILES):
                split_hi(t, t, 16)
            act.wait_ge(qkv_ready, 1)
            for half in range(KT):
                last = nc.scalar.activation(kTs[:, half, :], sc[1][:, 512 + half * TOK:512 + (half + 1) * TOK],
                                            ACT.Identity, bias=bqk_sb[:, KT + half:KT + half + 1])
            last.then_inc(kT_plain, 1)
            act.wait_ge(kT_plain, 1)
            act.wait_ge(own_done, 3)
            k_by_b = kTs[:, :, :].rearrange("p k (b n) -> p b k n", b=B)
            for j in range(KBD_DVE, P // SD):
                last = nc.scalar.activation(kbd[:, :, :, j, :], k_by_b, ACT.Copy, scale=own_rows[:, j:j + 1])
            last.then_inc(kbd_ready, 1)
            units = B * SQ
            for u in range(units + 1):
                if u < units:
                    act.wait_ge(s_shifted, u + 1)
                    if u >= 2:
                        act.wait_ge(p_turned, u - 1)
                    nc.scalar.activation(sprob[:, u % 2, :], ssub[:, u % 2, :], ACT.Exp).then_inc(s_exp, 1)
                if u >= 1:
                    act.wait_ge(p_turned, u)
                    if u >= 3:
                        act.wait_ge(o_ready, u - 2)
                    nc.scalar.activation(sprobT[:, (u - 1) % 2, :], pj[(u - 1) % 2][:, :], ACT.Copy).then_inc(pT_ready, 1)

            act.wait_ge(hT_ready, 3)
            nc.scalar.activation(xT_hl[:, 0, :, :], hT[:, :, :], ACT.Copy, scale=X_UP).then_inc(xhi_ready, 1)
            act.wait_ge(logits_shifted, 1)
            nc.scalar.activation(comb[:, :, :], comb[:, :, :], ACT.Exp).then_inc(gate_exp, 1)

            def silu(s, t):
                act.wait_ge(up_ready, t + 1)
                if not (isinstance(t, int) and t < 2):
                    act.wait_ge(weighed, t - 1)
                slot = s % SLOTS
                nc.scalar.activation(sil[:, s % 2, :], sc[slot // 2][:, slot % 2 * 512:slot % 2 * 512 + TOK],
                                     ACT.Silu, scale=1.0 / (W_UP * X_UP)).then_inc(sil_ready, 1)

            def split_act_hi(s, t):
                act.wait_ge(weighed, t + 1)
                nc.scalar.activation(act_hl[:, s % SLOTS, 0, :], act_sb[:, s % 2, :], ACT.Copy).then_inc(ahi_ready, 1)

            for t in range(SLOTS + 2):
                silu(t, t)
                if t + 2 >= SHARED_TILES:
                    split_hi(t + 2, t + 2, 16 * (1 + (t + 2) // SLOTS))
                split_act_hi(t, t)
            with act.Fori(1, TILES // SLOTS - 1) as i:
                for s in range(2, 2 + SLOTS):
                    silu(s, SLOTS * i + s)
                    split_hi(s + 2, SLOTS * i + s + 2, 16 * i + 16 * (1 + (s + 2) // SLOTS))
                    split_act_hi(s, SLOTS * i + s)
            for t in range(TILES // SLOTS * SLOTS - 2, TILES):
                silu(t, t)
                if t + 2 < TILES:
                    split_hi(t + 2, t + 2, 16 * (1 + (t + 2) // SLOTS))
                split_act_hi(t, t)

        @block.vector
        def _(dve):
            step = Steps(dve, dve_step)
            v = nc.vector

            def newton_by_column(n):
                x_, h_, t_, y_ = (a[:, 0:n] for a in (rs_x, rs_h, rs_t, rs_y))
                step(v.tensor_scalar(h_, x_, -0.5, None, ALU.mult))
                step.then(v.tensor_scalar(t_.bitcast(U32), x_.bitcast(U32), 1, 0x7FFFFFFF,
                                          ALU.logical_shift_right, ALU.bitwise_xor))
                step.then(v.tensor_scalar(y_, t_, SEED, None, ALU.mult))
                for _ in range(3):
                    for c in range(n):
                        step(v.scalar_tensor_tensor(out=t_[:, c:c + 1], in0=y_[:, c:c + 1], scalar=h_[:, c:c + 1],
                                                    in1=y_[:, c:c + 1], op0=ALU.mult, op1=ALU.mult))
                    step.wait()
                    step.then(v.scalar_tensor_tensor(out=y_, in0=t_, scalar=1.5, in1=y_, op0=ALU.add, op1=ALU.mult))

            def layernorm(first=False):
                for b in range(B):
                    step(v.bn_stats(stats[:, b, :], xres[:, b, :]))
                step.wait()
                for b in range(B):
                    step(v.bn_aggr(mv[:, b, :], stats[:, b, :]))
                step.wait()
                if first:
                    v.tensor_scalar(rs_t[:, 0:B], mv[:, :, 1], LN_EPS, None, ALU.add).then_inc(sums_ready, 1)
                    dve.wait_ge(roots_ready, 1)
                    step.then(v.reciprocal(rs_y[:, 0:B], rs_x[:, 0:B]))
                else:
                    step.then(v.tensor_scalar(rs_x[:, 0:B], mv[:, :, 1], LN_EPS, None, ALU.add))
                    newton_by_column(B)
                for b in range(B):
                    last = v.tensor_scalar(h[:, b, :], xres[:, b, :], mv[:, b, 0:1], rs_y[:, b:b + 1],
                                           ALU.subtract, ALU.mult)
                last.then_inc(h_ready, 1)

            def take_hT(n, turned, ready):
                dve.wait_ge(turned, n)
                v.tensor_copy(hT[:, :, :].rearrange("p k t -> p (k t)"), sc[0][:, 0:512]).then_inc(ready, 1)

            def ask_roots(sq, heads):
                step.then(v.tensor_reduce(rs_h[:, 0:heads], sq.rearrange("p (h d) -> p h d", d=XD), AX, ALU.add))
                v.tensor_scalar(rs_t[:, 0:heads], rs_h[:, 0:heads], 1.0 / XD, RMS_EPS, ALU.mult,
                                ALU.add).then_inc(sums_ready, 1)

            def normalise(nth, raw, hi_lo, heads, lo_at):
                dve.wait_ge(roots_ready, nth)
                step.then(v.reciprocal(rs_y[:, 0:heads], rs_x[:, 0:heads]))
                n3 = kn[:, 0:heads * XD].rearrange("p (h d) -> p h d", d=XD)
                step.then(v.scalar_tensor_tensor(out=n3, in0=raw.rearrange("p (h d) -> p h d", d=XD), scalar=QK_UP,
                                                 in1=rs_y[:, 0:heads].unsqueeze(2).broadcast_to([P, heads, XD]),
                                                 op0=ALU.mult, op1=ALU.mult))
                step.then(v.tensor_copy(hi_lo[:, :, 0:XD], n3))
                step.then(v.tensor_tensor(hi_lo[:, :, lo_at:lo_at + XD], n3, hi_lo[:, :, 0:XD], ALU.subtract))

            def split_ctx(slot, grp, loads):
                dve.wait_ge(ctx_in[slot], loads)
                if not (isinstance(grp, int) and grp < 2):
                    dve.wait_ge(kv_ready, GRP * (grp - 1))
                src = ctx_in_sb[:, slot, :, :].rearrange("p k n -> p (k n)")
                step.then(v.tensor_scalar(ctx_hl[:, slot, 0, :], src, CTX_UP, None, ALU.mult))
                v.scalar_tensor_tensor(out=ctx_hl[:, slot, 1, :], in0=src, scalar=CTX_UP, in1=ctx_hl[:, slot, 0, :],
                                       op0=ALU.mult, op1=ALU.subtract).then_inc(ctx_lo, 1)

            step(v.memset(ones_row[:, :], 1.0))
            dve.wait_ge(ident_done, 1)
            step(v.tensor_copy(ident_h[:, :], ident[:, :]))
            idv = ident[:, :].rearrange("p (t half n) -> p t half n", t=2, half=2)
            for ab in range(2):
                step(v.tensor_tensor(pick[:, ab, :, :], idv[:, :, 0, ab * VW:(ab + 1) * VW],
                                     idv[:, :, 1, ab * VW:(ab + 1) * VW], ALU.add))

            dve.wait_ge(x_in, 16)
            layernorm(first=True)
            dve.wait_ge(wkv_hi, 1)
            v.scalar_tensor_tensor(out=wkv_hl[:, 1, :, :].rearrange("p k n -> p (k n)"),
                                   in0=wkv_sb[:, :, :].rearrange("p k n -> p (k n)"), scalar=WKV_UP,
                                   in1=wkv_hl[:, 0, :, :].rearrange("p k n -> p (k n)"),
                                   op0=ALU.mult, op1=ALU.subtract).then_inc(wkv_lo, 1)
            split_ctx(0, 0, 16)
            split_ctx(1, 1, 16)
            take_hT(1, hT_turned, hT_ready)
            dve.wait_ge(q_ready, 1)
            step.then(v.tensor_copy(q_raw, sc[1][:, 0:B * D]))
            step.then(v.tensor_tensor(q_sq, q_raw, q_raw, ALU.mult))
            ask_roots(q_sq, B * XH)
            normalise(2, q_raw, q32, B * XH, 2 * XD)
            q_halves = q32.rearrange("p h (half two d) -> p h half two d", half=2, two=2)
            v.tensor_copy(q_halves[:, :, :, 1, :], q_halves[:, :, :, 0, :]).then_inc(q_normed, 1)
            def spread_queries():
                dve.wait_ge(ident_done, 2)
                for b in range(B):
                    dve.wait_ge(q_turned, b + 1)
                    src = (turn_bank, av)[b][:, :].bitcast(F16).rearrange("p (g n) -> p g n", g=NG)
                    for j in range(4):
                        last = v.tensor_copy(qbd[32 * j:32 * j + 32, :, b, j * P:(j + 1) * P],
                                             src[32 * j:32 * j + 32, :, :])
                    last.then_inc(q_taken, 1)

            def ask_key_roots(slot, grp):
                dve.wait_ge(kv_taken, GRP * grp + GRP)
                ask_roots(ksq[:, slot, :], GRP * XH)

            def normalise_keys(slot, grp):
                if not (isinstance(grp, int) and grp < 2):
                    dve.wait_ge(turned, GRP * grp - GRP)
                normalise(grp + 3, kraw[:, slot, :], k32[:, slot, :, :], GRP * XH, XD)
                v.tensor_copy(k32[:, slot, :, 2 * XD:], k32[:, slot, :, 0:2 * XD]).then_inc(normed, 1)

            for grp in range(GROUPS - 1):
                ask_key_roots(grp % 2, grp)
                if grp + 2 < GROUPS:
                    split_ctx(grp % 2, grp + 2, 16 * (1 + (grp + 2) // 2))
                normalise_keys(grp % 2, grp)
                if grp == 0:
                    spread_queries()

            def stage(b, g):
                v.tensor_copy(k_stage[:, b, :], kT[:, bass.ds(g, 1), b * CTX:(b + 1) * CTX].rearrange(
                    "p g n -> p (g n)"))
                v.tensor_copy(v_stage[:, b, :, :].rearrange("p c n -> p (c n)"),
                              v_all[:, bass.ds(g, 1), b * CPB:(b + 1) * CPB, :].rearrange("p g c n -> p (g c n)"))
                v.tensor_copy(q_stage[:, b, :], qbd[:, bass.ds(g, 1), b, :].rearrange(
                    "p g n -> p (g n)")).then_inc(staged, 1)

            def take_av(b, g):
                dve.wait_ge(av_ready, 2 * g + b + 1)
                src, to = pj[b][:, 0:2 * P], av_hl[:, bass.ds(2 * g + b, 1), :, :]
                hi, lo = (to[:, :, half, :].rearrange("p u n -> p (u n)") for half in range(2))
                step.then(v.tensor_scalar(hi, src, AV_DOWN, None, ALU.mult))
                v.scalar_tensor_tensor(out=lo, in0=src, scalar=AV_DOWN, in1=hi, op0=ALU.mult,
                                       op1=ALU.subtract).then_inc(av_taken, 1)

            ask_key_roots(1, GROUPS - 1)
            for b in range(B):
                v.memset(pj[b][:, :], 0.0)
            dve.wait_ge(kv_ready, CHUNKS)
            dve.wait_ge(turn_free, CPB)
            stage(0, 0)
            normalise_keys(1, GROUPS - 1)
            dve.wait_ge(turn_free, CHUNKS)
            stage(1, 0)
            with dve.Fori(0, NG - 1) as g:
                step.enter(g, 0, B)
                for b in range(B):
                    take_av(b, g)
                    stage(b, g + 1)
            step.leave(NG - 1)
            for b in range(B):
                take_av(b, NG - 1)
            for b in range(B):
                dve.wait_ge(merged, b + 1)
                got = (turn_bank, av)[b][:, 0:XH * VW].rearrange("p (g ab t d) -> p g t ab d", g=NG, ab=2, t=2)
                rec = srec[:, b, :].rearrange("p (g t ab) -> p g t ab", g=NG, t=2)
                step.then(v.reciprocal(rec, got[:, :, :, :, XD]))
                new = h[:, b, :].rearrange("p (g t ab d) -> p g t ab d", g=NG, t=2, ab=2)
                for ab in range(2):
                    step(v.tensor_tensor(new[:, :, :, ab, :], got[:, :, :, ab, 0:XD],
                                         rec[:, :, :, ab].unsqueeze(3).broadcast_to([P, NG, 2, XD]), ALU.mult))
                step.wait()
                step.then(v.tensor_tensor(xres[:, b, :], xres[:, b, :], h[:, b, :], ALU.add))

            layernorm()
            take_hT(2, hT_turned, hT_ready)
            def split_lo(s, t):
                slot = s % SLOTS
                dve.wait_ge(whi_ready, t + 1)
                v.scalar_tensor_tensor(out=w_hl[:, slot, 1, :], in0=ring[:, slot, :], scalar=W_UP,
                                       in1=w_hl[:, slot, 0, :], op0=ALU.mult, op1=ALU.subtract).then_inc(wlo_ready, 1)

            for t in range(SHARED_TILES):
                split_lo(t, t)
            v.memset(sv[:, :, :, SD:SVW], 1.0)
            dve.wait_ge(own_done, 3)
            dve.wait_ge(kT_plain, 1)
            k_by_b = kTs[:, :, :].rearrange("p k (b n) -> p b k n", b=B)
            for j in range(KBD_DVE):
                last = v.tensor_scalar(kbd[:, :, :, j, :], k_by_b, own_rows[:, j:j + 1], None, ALU.mult)
            last.then_inc(kbd_ready, 1)
            dve.wait_ge(qkv_ready, 2)
            for half in range(KT):
                last = v.tensor_scalar(qT[:, half, :], sc[1][:, half * TOK:(half + 1) * TOK],
                                       bqk_sb[:, half:half + 1], SD ** -0.5, ALU.add, ALU.mult)
            last.then_inc(qT_ready, 1)
            dve.wait_ge(qkv_ready, 3)
            v.tensor_copy(sv[:, :, :, 0:SD], pj[0][:, :].rearrange("p (b h d) -> p b h d", b=B, h=SH)).then_inc(sv_ready, 1)
            for u in range(B * SQ):
                dve.wait_ge(s_ready, u + 1)
                src = sc[u // 2 % 2][:, u % 2 * 512:(u % 2 + 1) * 512].rearrange("p (h n) -> p h n", h=4)
                top = smax[:, u % 2 * 4:u % 2 * 4 + 4]
                step.then(v.tensor_reduce(top, src, AX, ALU.max))
                if u >= 2:
                    dve.wait_ge(s_exp, u - 1)
                v.tensor_tensor(ssub[:, u % 2, :].rearrange("p (h n) -> p h n", h=4), src,
                                top.unsqueeze(2).broadcast_to([P, 4, P]), ALU.subtract).then_inc(s_shifted, 1)
            for b in range(B):
                dve.wait_ge(o_ready, SQ * (b + 1))
                got = (turn_bank, av)[b][:, 0:SH * SVW].rearrange("p (h d) -> p h d", d=SVW)
                step.then(v.reciprocal(srec[:, b, 0:SH], got[:, :, SD]))
                last = v.tensor_tensor(h[:, b, :].rearrange("p (h d) -> p h d", d=SD), got[:, :, 0:SD],
                                       srec[:, b, 0:SH].unsqueeze(2).broadcast_to([P, SH, SD]), ALU.mult)
            last.then_inc(o_norm, 1)
            take_hT(1, oT_turned, oT_ready)
            dve.wait_ge(y_ready, 1)
            xflat = xres[:, :, :].rearrange("p b n -> p (b n)")
            step.then(v.tensor_tensor(xflat, xflat, pj[1][:, :], ALU.add))

            layernorm()
            take_hT(3, hT_turned, hT_ready)
            step(v.memset(ppad[:, :, E:E + 1], -1.0))
            step(v.memset(ppad[:, :, E + 1:E + 2], -2.0))
            step(v.memset(topk[:, :, TOPK:TOPK + 1], -1.0))
            step(v.memset(topk[:, :, TOPK + 1:TOPK + 2], -2.0))
            dve.wait_ge(xhi_ready, 1)
            v.scalar_tensor_tensor(out=xT_hl[:, 1, :, :].rearrange("p k t -> p (k t)"),
                                   in0=hT[:, :, :].rearrange("p k t -> p (k t)"), scalar=X_UP,
                                   in1=xT_hl[:, 0, :, :].rearrange("p k t -> p (k t)"),
                                   op0=ALU.mult, op1=ALU.subtract).then_inc(xlo_ready, 1)

            def over_experts(a):
                return a.unsqueeze(2).broadcast_to([P, B, E])

            dve.wait_ge(logits_ready, 1)
            lg = turn_bank[:, 0:B * E].rearrange("p (b e) -> p b e", b=B)
            top, total, part = rstat[:, 0, :], rstat[:, 1, :], rstat[:, 2, :]
            p_in = ppad[:, :, 0:E]
            step.then(v.tensor_reduce(top, lg, AX, ALU.max))
            v.tensor_tensor(comb[:, :, :], lg, over_experts(top), ALU.subtract).then_inc(logits_shifted, 1)
            dve.wait_ge(gate_exp, 1)
            step.then(v.tensor_reduce(total, comb[:, :, :], AX, ALU.add))
            step.then(v.reciprocal(total, total))
            step.then(v.tensor_tensor(p_in, comb[:, :, :], over_experts(total), ALU.mult))
            for b in range(B):
                step(v.max(top8[:, b, :], ppad[:, b, :]))
            step.wait()
            step.then(v.tensor_copy(topk[:, :, 0:TOPK], top8[:, :, 0:TOPK]))
            step(v.tensor_reduce(part, topk[:, :, 0:TOPK], AX, ALU.add))
            for b in range(B):
                step(v.match_replace(out=prep[:, b, :], in_to_replace=topk[:, b, :], in_values=ppad[:, b, :],
                                     imm_value=-3.0))
            step.wait()
            step(v.tensor_scalar(part, part, TOPK_EPS, 1.0 / COMB_UP, ALU.add, ALU.mult))
            step.then(v.tensor_tensor(prep[:, :, 0:E], p_in, prep[:, :, 0:E], ALU.not_equal))
            step(v.reciprocal(part, part))
            step.then(v.tensor_tensor(prep[:, :, 0:E], p_in, prep[:, :, 0:E], ALU.mult))
            step.then(v.tensor_tensor(comb[:, :, :], prep[:, :, 0:E], over_experts(part), ALU.mult))
            step.then(v.tensor_copy(comb_hl[:, :, 0, :], comb[:, :, :]))
            v.tensor_tensor(comb_hl[:, :, 1, :], comb[:, :, :], comb_hl[:, :, 0, :],
                            ALU.subtract).then_inc(comb_ready, 1)
            dve.wait_ge(comb_turned, 1)
            v.tensor_copy(combT[:, :], av[:, :].bitcast(F16)[:, 0:TOK]).then_inc(combT_ready, 1)

            def gate_up(s, t, routed=True):
                slot = s % SLOTS
                upv = sc[slot // 2][:, slot % 2 * 512 + TOK:(slot % 2 + 1) * 512]
                dve.wait_ge(sil_ready, t + 1)
                share = COMB_UP if routed else 1.0
                to = gated if routed else act_sb
                first = v.scalar_tensor_tensor(out=to[:, s % 2, :], in0=upv, scalar=ACT_UP / (W_UP * X_UP * share),
                                               in1=sil[:, s % 2, :], op0=ALU.mult, op1=ALU.mult)
                if routed:
                    step.then(first)
                    v.tensor_tensor(act_sb[:, s % 2, :], gated[:, s % 2, :], (turn_bank, av)[s % 2][:, 0:TOK],
                                    ALU.mult).then_inc(weighed, 1)
                else:
                    first.then_inc(weighed, 1)

            def split_act_lo(s, t):
                slot = s % SLOTS
                dve.wait_ge(ahi_ready, t + 1)
                v.tensor_tensor(act_hl[:, slot, 1, :], act_sb[:, s % 2, :], act_hl[:, slot, 0, :],
                                ALU.subtract).then_inc(alo_ready, 1)

            for t in range(SLOTS + 2):
                gate_up(t, t, t >= SHARED_TILES)
                if t + 2 >= SHARED_TILES:
                    split_lo(t + 2, t + 2)
                split_act_lo(t, t)
            with dve.Fori(1, TILES // SLOTS - 1) as i:
                step.enter(i, 1, SLOTS)
                for s in range(2, 2 + SLOTS):
                    gate_up(s, SLOTS * i + s)
                    split_lo(s + 2, SLOTS * i + s + 2)
                    split_act_lo(s, SLOTS * i + s)
            step.leave(TILES // SLOTS - 2)
            for t in range(TILES // SLOTS * SLOTS - 2, TILES):
                gate_up(t, t)
                if t + 2 < TILES:
                    split_lo(t + 2, t + 2)
                split_act_lo(t, t)
            dve.wait_ge(down_done, TILES)
            for b in range(B):
                last = v.scalar_tensor_tensor(out=final[:, b, :], in0=pj[b][:, 0:D], scalar=1.0 / (W_UP * ACT_UP),
                                              in1=xres[:, b, :], op0=ALU.mult, op1=ALU.add)
            last.then_inc(final_ready, 1)


def kernel(**inputs):
    import numpy as np
    import concourse.bacc as bacc
    from concourse.bass_utils import run_bass_kernel_spmd

    a = {k: np.asarray(v) for k, v in inputs.items()}

    def kparts(w):
        return np.ascontiguousarray(w.reshape(KT, P, -1).transpose(1, 0, 2))

    arrays = {"x": np.ascontiguousarray(a["x"].transpose(1, 0, 2))}
    arrays["ctxT"] = kparts(a["ctx_2048"].reshape(B * CTX, D).T)
    arrays["wq"] = kparts(a["L0_xattn_Wq"].T)
    w = np.concatenate([a["L0_xattn_Wk"], a["L0_xattn_Wv"]]).reshape(D, 2, D)
    arrays["wkv"] = kparts(np.concatenate([w[:, 0].T, w[:, 1].T], axis=1))
    wqkv = a["L0_attn_W_qkv"].reshape(D, SH, 3, SD)
    bqkv = a["L0_attn_b_qkv"].reshape(SH, 3, SD)
    arrays["wqk"] = kparts(wqkv[:, :, :2].transpose(0, 2, 1, 3).reshape(D, -1)).reshape(P, KT, 2 * KT, P)
    arrays["bqk"] = np.ascontiguousarray(bqkv[:, :2].transpose(1, 0, 2).reshape(2 * KT, P).T)
    arrays["wsv"] = kparts(wqkv[:, :, 2].reshape(D, D))
    arrays["bv"] = np.ascontiguousarray(bqkv[:, 2].reshape(1, D))
    arrays["wout"] = kparts(a["L0_attn_W_out"])
    arrays["bout"] = a["L0_attn_b_out"].reshape(1, D)
    arrays["gate"] = kparts(a["L0_ffn_gate_w"].T)
    gu, dn = a["L0_ffn_w_gate_up"], a["L0_ffn_w_down"]
    sgu, sdn = a["L0_ffn_ws_gate_up"], a["L0_ffn_ws_down"]
    moe = np.zeros((TILES, P, TILE_W), gu.dtype)
    for n, (routed, shared) in enumerate(((gu[:, :FFN], sgu[:2 * FFN]), (gu[:, FFN:], sgu[2 * FFN:]))):
        rows = np.zeros((TILES * P, D), gu.dtype)
        rows[:2 * FFN] = shared
        rows[SHARED_TILES * P:] = routed.reshape(-1, D)
        moe[:, :, n * KT * P:(n + 1) * KT * P] = rows.reshape(TILES, P, KT, P).transpose(0, 3, 2, 1).reshape(
            TILES, P, KT * P)
    rows = np.zeros((TILES * P, D), gu.dtype)
    rows[:2 * FFN] = sdn.T
    rows[SHARED_TILES * P:] = dn.transpose(0, 2, 1).reshape(-1, D)
    moe[:, :, 2 * KT * P:] = rows.reshape(TILES, P, D)
    arrays["moe"] = moe

    nc = bacc.Bacc("TRN2", target_bir_lowering=False, num_devices=1)
    order = ["x", "ctxT", "wq", "wkv", "wqk", "wsv", "bqk", "bv", "wout", "bout", "gate", "moe"]
    args = [nc.dram_tensor(f"{n}_dram", arrays[n].shape, F32, kind="ExternalInput").ap() for n in order]
    out = nc.dram_tensor("out_dram", (P, B, D), F32, kind="ExternalOutput").ap()
    perceiver(nc, *args, out)
    r = run_bass_kernel_spmd(nc, [{f"{n}_dram": arrays[n] for n in order}], core_ids=[0])
    return np.ascontiguousarray(r.results[0]["out_dram"].transpose(1, 0, 2))
```

```python
from contextlib import ExitStack

import concourse.bass as bass
from concourse import mybir

P = 128
B = 2
D = 256
KT = D // P
TOK = B * P
CTX = 2048
XH, XD = 32, 8
NG = XH // 4
CHUNKS = B * CTX // P
GRP = 4
GROUPS = CHUNKS // GRP
CPB = CTX // P
PAIRS = CPB // 2
VW = XD + 1
SH, SD = 16, 16
SQ = SH // 4
SVW = SD + 1
E, FFN, TOPK = 64, 176, 6
ROUTED_TILES = E * FFN // P
SHARED_TILES = 3
TILES = ROUTED_TILES + SHARED_TILES
TILE_W = 2 * KT * P + D
RING = 8
SLOTS = 4
LN_EPS, RMS_EPS, TOPK_EPS = 1e-5, 1e-6, 1e-20
QK_UP = 64.0
TURN_AT = 3
AV_DOWN = 2.0 ** -6
COMB_UP = 1024.0
W_UP = 64.0
X_UP = 16.0
ACT_UP = 16.0
CTX_UP = 16.0
WKV_UP = 64.0
SEED = 0.68 * 2.0 ** -65

ALU = mybir.AluOpType
ACT = mybir.ActivationFunctionType
AX = mybir.AxisListType.X
F32 = mybir.dt.float32
F16 = mybir.dt.float16
U32 = mybir.dt.uint32


UNITS = [(0, 0), (0, 1)]
for _g in range(NG - 2):
    UNITS += [(1, _g), (0, _g + 2)]
UNITS += [(1, NG - 2), (1, NG - 1)]


class Steps:

    def __init__(self, eng, sem):
        self.eng, self.sem, self.base, self.n = eng, sem, 0, 0

    def __call__(self, ins):
        ins.then_inc(self.sem, 1)
        self.n += 1

    def wait(self):
        self.eng.wait_ge(self.sem, self.base + self.n)

    def wait_older(self, younger):
        self.eng.wait_ge(self.sem, self.base + self.n - younger)

    def then(self, ins):
        self(ins)
        self.wait()

    def enter(self, i, first, per_turn):
        self.start, self.per = self.base + self.n, per_turn
        self.base, self.n = self.start - first * per_turn + i * per_turn, 0

    def leave(self, turns):
        assert self.n == self.per, (self.n, self.per)
        self.base, self.n = self.start + turns * self.per, 0


def perceiver(nc, x, ctxT, wq, wkv, wqk, wsv, bqk, bv, wout, bout, gate, moe, out):
    with ExitStack() as stack:
        def sb(name, shape, dt=F32):
            return stack.enter_context(nc.sbuf_tensor(name, shape, dt))

        def ps(name, shape, dt=F32):
            return stack.enter_context(nc.psum_tensor(name, shape, dt))

        def sem(name):
            return stack.enter_context(nc.semaphore(name))

        sc = [ps("scores0", [P, 1024]), ps("scores1", [P, 1024])]
        pj = [ps("proj0", [P, 512]), ps("proj1", [P, 512])]
        turn_bank = ps("turn", [P, 512])
        av = ps("av", [P, 512])

        ident = sb("ident", [P, P])
        ident_h = sb("ident_h", [P, P], F16)
        pick = sb("pick", [P, 2, 2, VW], F16)
        wq_sb = sb("wq_sb", [P, KT, D])
        wkv_sb = sb("wkv_sb", [P, KT, 2 * D])
        wkv_hl = sb("wkv_hl", [P, 2, KT, 2 * D], F16)
        wqk_sb = sb("wqk_sb", [P, KT, 2 * KT, P])
        wsv_sb = sb("wsv_sb", [P, KT, D])
        bqk_sb = sb("bqk_sb", [P, 2 * KT])
        eps_sb = sb("eps_sb", [P, 2])
        table_out = sb("table_out", [P, 5])
        own_rows = sb("own_rows", [P, P // SD])
        own_bias = sb("own_bias", [P, P // SD])
        bv_sb = sb("bv_sb", [P, D])
        wout_sb = sb("wout_sb", [P, KT, D])
        bout_sb = sb("bout_sb", [P, D])
        gate_sb = sb("gate_sb", [P, KT, E])
        xres = sb("xres", [P, B, D])
        h = sb("h", [P, B, D])
        hT = sb("hT", [P, KT, TOK])
        ln_eps, rms_eps = (eps_sb[:, n:n + 1] for n in range(2))
        stats = sb("stats", [P, B, 6])
        mv = sb("mv", [P, B, 2])
        rs_x = sb("rs_x", [P, GRP * XH])
        rs_h = sb("rs_h", [P, GRP * XH])
        rs_t = sb("rs_t", [P, GRP * XH])
        rs_y = sb("rs_y", [P, GRP * XH])
        early = sb("early", [P, 9 * GRP * D + GRP * XH * 4 * XD // 2 * 2])

        def carve(space):
            taken = [0]

            def room(n):
                taken[0] += n
                assert taken[0] <= space.shape[1], (taken, space.shape)
                return space[:, taken[0] - n:taken[0]]
            return room

        HALVES = ((0, 0), (0, 1), (1, 0))

        room = carve(early[:, :])
        ctx_in_sb = room(2 * KT * GRP * P).rearrange("p (s k n) -> p s k n", s=2, k=KT)
        ctx_hl = room(2 * KT * GRP * P).bitcast(F16).rearrange("p (s two n) -> p s two n", s=2, two=2)
        ksq = room(2 * GRP * D).rearrange("p (s n) -> p s n", s=2)
        kraw = room(2 * GRP * D).rearrange("p (s n) -> p s n", s=2)
        kn = room(GRP * D)
        k32 = room(GRP * XH * 4 * XD).bitcast(F16).rearrange("p (s h r) -> p s h r", s=2, h=GRP * XH)
        kT = sb("kT", [P, NG, B * CTX], F16)
        v_all = sb("v_all", [P, NG, CHUNKS, 4 * VW])
        q_all = sb("q_all", [P, NG, B, P], F16)
        room = carve(early[:, :])
        k_stage = room(CTX).bitcast(F16).rearrange("p (s n) -> p s n", s=2)
        v_stage = sb("v_stage", [P, 2, CPB, 4 * VW])
        q_stage = sb("q_stage", [P, 2, 4 * P], F16)
        q_sq = q_stage[:, :, :].rearrange("p b n -> p (b n)").bitcast(F32)
        q32 = v_stage[:, :, :, :].rearrange("p b c n -> p (b c n)").bitcast(F16)[:, 0:B * XH * 4 * XD].rearrange(
            "p (h r) -> p h r", h=B * XH)
        q_raw = h[:, :, :].rearrange("p b n -> p (b n)")
        probs = room(4 * 1024).rearrange("p (u n) -> p u n", u=4)
        av_hl = room(2 * NG * 2 * P).bitcast(F16).rearrange("p (u two n) -> p u two n", u=2 * NG, two=2)

        early_room = room
        room = carve(kT[:, :, :].rearrange("p g n -> p (g n)").bitcast(F32))
        qT = room(KT * TOK).rearrange("p (k t) -> p k t", k=KT)
        self_k = [sc[1][:, 0:TOK], sc[1][:, 512:512 + TOK]]
        self_q = [sc[0][:, 512:512 + TOK], sc[0][:, 512 + TOK:1024]]
        kbd = room(B * SH * P).rearrange("p (b k j n) -> p b k j n", b=B, k=KT, j=P // SD)
        sv = room(B * SH * SVW).rearrange("p (b h d) -> p b h d", b=B, h=SH)
        so = room(2 * P).rearrange("p (u n) -> p u n", u=2)
        sprob = room(2 * 512).rearrange("p (u n) -> p u n", u=2)
        sprobT = room(2 * 512).rearrange("p (u n) -> p u n", u=2)
        vroom = v_all[:, :, :, :].rearrange("p g c n -> p (g c n)")
        ring = early[:, 0:RING * TILE_W].rearrange("p (s n) -> p s n", s=RING)
        onehot = vroom.bitcast(F16)[:, 0:E * FFN]
        less_top = sb("less_top", [P, B * SH])
        srec = sb("srec", [P, B, XH])
        ppad = sb("ppad", [P, B, E + 2])
        prep = sb("prep", [P, B, E + 2])
        top8 = sb("top8", [P, B, 8])
        topk = sb("topk", [P, B, 8])
        rstat = sb("rstat", [P, 4, B])
        comb = sb("comb", [P, B, E])
        comb_hl = sb("comb_hl", [P, B, 2, E], F16)
        combT = sb("combT", [P, TOK], F16)
        sil = early_room(2 * TOK).rearrange("p (u t) -> p u t", u=2)
        gated = room(2 * TOK).rearrange("p (u t) -> p u t", u=2)
        act_sb = room(2 * TOK).rearrange("p (u t) -> p u t", u=2)
        act_hl = room(SLOTS * TOK).bitcast(F16).rearrange("p (u two t) -> p u two t", u=SLOTS, two=2)
        xT_hl = room(KT * TOK).bitcast(F16).rearrange("p (two k t) -> p two k t", two=2, k=KT)
        w_hl = room(RING * TILE_W).bitcast(F16).rearrange("p (s two n) -> p s two n", s=RING, two=2)
        final = h

        x_in, wq_in, wkv_in, attn_in, y_out = (sem(n) for n in ("x_in", "wq_in", "wkv_in", "attn_in", "y_out"))
        ctx_in = [sem("ctx_in0"), sem("ctx_in1")]
        moe_in = [sem(f"moe_in{s}") for s in range(RING)]
        half_in = sem("half_in")
        ident_zero, ident_done, onehot_step = sem("ident_zero"), sem("ident_done"), sem("onehot_step")
        dve_step = sem("dve_step")
        act_step = sem("act_step")
        h_ready, hT_turned, hT_first, hT_ready = (sem(n) for n in ("h_ready", "hT_turned", "hT_first", "hT_ready"))
        q_ready, q_normed, q_turned, q_taken = (sem(n) for n in ("q_ready", "q_normed", "q_turned", "q_taken"))
        q_out, q_cleared = sem("q_out"), sem("q_cleared")
        kv_ready, kv_taken = sem("kv_ready"), sem("kv_taken")
        wkv_hi, wkv_lo, ctx_lo = (sem(n) for n in ("wkv_hi", "wkv_lo", "ctx_lo"))
        eps_set = sem("eps_set")
        sums_ready, roots_ready = sem("sums_ready"), sem("roots_ready")
        normed, turned, turn_free = sem("normed"), sem("turned"), sem("turn_free")
        staged, scores_ready, probs_ready = sem("staged"), sem("scores_ready"), sem("probs_ready")
        sums_cleared, last_taken = sem("sums_cleared"), sem("last_taken")
        av_ready, av_taken, merged = sem("av_ready"), sem("av_taken"), sem("merged")
        qkv_ready, qT_ready, own_biased, sv_ready = (
            sem(n) for n in ("qkv_ready", "qT_ready", "own_biased", "sv_ready"))
        kbd_ready = [sem("kbd_ready0"), sem("kbd_ready1")]
        s_ready, s_topped, s_exp, p_turned, pT_ready, o_ready, o_out, o_back = (
            sem(n) for n in ("s_ready", "s_topped", "s_exp", "p_turned", "pT_ready", "o_ready", "o_out", "o_back"))
        o_norm, oT_turned, oT_ready, y_ready = sem("o_norm"), sem("oT_turned"), sem("oT_ready"), sem("y_ready")
        logits_ready, logits_shifted, gate_exp, own_done = (
            sem(n) for n in ("logits_ready", "logits_shifted", "gate_exp", "own_done"))
        comb_ready, comb_turned, combT_ready = sem("comb_ready"), sem("comb_turned"), sem("combT_ready")
        xhi_ready, xlo_ready, whi_ready, wlo_ready = (sem(n) for n in ("xhi_ready", "xlo_ready", "whi_ready", "wlo_ready"))
        up_ready, sil_ready, weighed, ahi_ready, alo_ready, down_done = (
            sem(n) for n in ("up_ready", "sil_ready", "weighed", "ahi_ready", "alo_ready", "down_done"))
        final_ready = sem("final_ready")

        block = stack.enter_context(nc.Block())

        @block.sync
        def _(sp):
            def load_ctx(slot, grp):
                sp.dma_start(ctx_in_sb[:, slot, :, :], ctxT[:, :, bass.ts(grp, GRP * P)]).then_inc(ctx_in[slot], 16)

            sp.dma_start(xres[:, :, :], x).then_inc(x_in, 16)
            sp.dma_start(wkv_sb[:, :, :], wkv).then_inc(wkv_in, 16)
            load_ctx(0, 0)
            sp.dma_start(wq_sb[:, :, :], wq).then_inc(wq_in, 16)
            load_ctx(1, 1)
            for dst, src in ((wqk_sb[:, :, :, :], wqk), (wsv_sb[:, :, :], wsv), (bqk_sb[:, :], bqk), (bv_sb[:, :], bv.partition_broadcast(P)),
                             (wout_sb[:, :, :], wout), (bout_sb[:, :], bout.partition_broadcast(P)), (gate_sb[:, :, :], gate)):
                sp.dma_start(dst, src).then_inc(attn_in, 16)
            with sp.Fori(0, GROUPS // 2 - 1) as i:
                for slot in range(2):
                    sp.wait_ge(ctx_lo, 2 * i + slot + 1)
                    load_ctx(slot, 2 * i + 2 + slot)

            def load_tile(slot, t):
                sp.dma_start(ring[:, slot, :], moe[t, :, :]).then_inc(moe_in[slot], 16)

            sp.wait_ge(av_ready, 2 * NG)
            for t in range(RING):
                load_tile(t, t)
            sp.wait_ge(onehot_step, 3)
            sp.dma_start(onehot[E:P, :], onehot[0:E, :]).then_inc(half_in, 16)
            with sp.Fori(0, TILES // RING - 1) as i:
                for slot in range(RING):
                    sp.wait_ge(wlo_ready, RING * i + slot + 1)
                    load_tile(slot, RING * i + RING + slot)
            for t in range(TILES // RING * RING, TILES):
                sp.wait_ge(wlo_ready, t - RING + 1)
                load_tile(t % RING, t)
            sp.wait_ge(final_ready, 1)
            sp.dma_start(out, final[:, :, :]).then_inc(y_out, 16)
            sp.wait_ge(y_out, 16)

        @block.gpsimd
        def _(pool):
            nc.gpsimd.memset(ident[:, :], 0.0).then_inc(ident_zero, 1)
            pool.wait_ge(ident_zero, 1)
            nc.gpsimd.affine_select(out=ident[:, :], in_=ident[:, :], compare_op=ALU.not_equal, fill=1.0, base=0,
                                    pattern=[[-1, P]], channel_multiplier=1).then_inc(ident_done, 1)
            nc.gpsimd.memset(v_all[:, :, :, :].rearrange("p g c (h d) -> p (g c h) d", d=VW)[:, :, XD:VW],
                             1.0).then_inc(ident_done, 1)
            nc.gpsimd.memset(own_rows[:, :], 1.0).then_inc(own_done, 1)
            pool.wait_ge(own_done, 1)
            nc.gpsimd.affine_select(out=own_rows[:, :], in_=own_rows[:, :], compare_op=ALU.is_ge, fill=0.0, base=0,
                                    pattern=[[-SD, P // SD]], channel_multiplier=1).then_inc(own_done, 1)
            pool.wait_ge(own_done, 2)
            nc.gpsimd.affine_select(out=own_rows[:, :], in_=own_rows[:, :], compare_op=ALU.is_ge, fill=0.0,
                                    base=SD - 1, pattern=[[SD, P // SD]], channel_multiplier=-1).then_inc(own_done, 1)
            pool.wait_ge(sums_ready, 2)
            nc.gpsimd.memset(q_stage[:, :, :], 0.0).then_inc(q_cleared, 1)
            pool.wait_ge(av_taken, 2 * NG)
            nc.gpsimd.memset(onehot[0:E, :], 1.0).then_inc(onehot_step, 1)
            pool.wait_ge(onehot_step, 1)
            nc.gpsimd.affine_select(out=onehot[0:E, :], in_=onehot[0:E, :], compare_op=ALU.is_ge, fill=0.0, base=0,
                                    pattern=[[1, E * FFN]], channel_multiplier=-FFN).then_inc(onehot_step, 1)
            pool.wait_ge(onehot_step, 2)
            nc.gpsimd.affine_select(out=onehot[0:E, :], in_=onehot[0:E, :], compare_op=ALU.is_ge, fill=0.0,
                                    base=FFN - 1, pattern=[[-1, E * FFN]],
                                    channel_multiplier=FFN).then_inc(onehot_step, 1)

        @block.tensor
        def _(pe):
            def turn_h(n, src, ready, turned):
                pe.wait_ge(ready, n)
                for kt in range(KT):
                    for b in range(B):
                        last = nc.tensor.transpose(sc[0][:, (kt * B + b) * P:(kt * B + b + 1) * P],
                                                   src[:, b, kt * P:(kt + 1) * P], ident[:, :])
                last.then_inc(turned, 1)

            def rows(bank, b, w, width, at):
                o = bank[:, at:at + width]
                for kt in range(KT):
                    last = nc.tensor.matmul(o, hT[:, kt, b * P:(b + 1) * P], w[:, kt, :],
                                            start=(kt == 0), stop=(kt == KT - 1))
                return last

            def project(slot, grp, c):
                if c == 0:
                    pe.wait_ge(ctx_lo, grp + 1)
                if not (isinstance(grp, int) and grp == 0 and c < 2):
                    pe.wait_ge(kv_taken, grp * GRP + c - 1)
                for kt in range(KT):
                    for n, (ch, wh) in enumerate(HALVES):
                        at = kt * GRP * P + c * P
                        last = nc.tensor.matmul(pj[c % 2][:, :], ctx_hl[:, slot, ch, at:at + P], wkv_hl[:, wh, kt, :],
                                                start=(kt == 0 and n == 0), stop=(kt == KT - 1 and n == 2))
                last.then_inc(kv_ready, 1)

            def turn_keys(slot, grp, c):
                if c == 0:
                    pe.wait_ge(normed, grp + 1)
                if isinstance(grp, int) and grp == 0 and c < 2:
                    pe.wait_ge(q_taken, c + 1)
                elif isinstance(grp, int) and grp == GROUPS - 1 and c >= 2:
                    pe.wait_ge(last_taken, c - 1)
                else:
                    pe.wait_ge(turn_free, grp * GRP + c - 1)
                dst = (turn_bank, av)[c % 2][:, :].bitcast(F16)
                for g in range(NG):
                    src = k32[:, slot, c * XH + 4 * g:c * XH + 4 * g + 4, :].rearrange("p h r -> p (h r)")
                    last = nc.tensor.transpose(dst[:, g * P:(g + 1) * P], src, ident_h[:, :])
                last.then_inc(turned, 1)

            def keep_warm(n, bank=sc[1]):
                for _ in range(n):
                    nc.tensor.matmul(bank[:, 0:P], ident[:, :], ident[:, :], start=True, stop=True)

            pe.wait_ge(ident_done, 1)
            keep_warm(10)
            turn_h(1, h, h_ready, hT_turned)
            keep_warm(3)
            pe.wait_ge(hT_first, 1)
            pe.wait_ge(wq_in, 16)
            for b in range(B):
                last = rows(sc[1], b, wq_sb, D, at=b * D)
            last.then_inc(q_ready, 1)
            pe.wait_ge(wkv_lo, 1)
            for grp in range(2):
                for c in range(GRP):
                    project(grp, grp, c)
            pe.wait_ge(q_normed, 1)
            for b in range(B):
                dst = (turn_bank, av)[b][:, :].bitcast(F16)
                for g in range(NG):
                    src = q32[:, b * XH + 4 * g:b * XH + 4 * g + 4, :].rearrange("p h r -> p (h r)")
                    last = nc.tensor.transpose(dst[:, g * P:(g + 1) * P], src, ident_h[:, :])
                last.then_inc(q_turned, 1)

            def project_and_turn(i):
                for slot in range(2):
                    for c in range(GRP):
                        project(slot, 2 * i + slot, c)
                        turn_keys(slot, 2 * i + slot - 2, c)

            project_and_turn(1)
            with pe.Fori(2, GROUPS // 2) as i:
                project_and_turn(i)
            for c in range(GRP):
                turn_keys(0, GROUPS - 2, c)

            def scores(slot, cp):
                for half in range(2):
                    c = 2 * cp + half
                    last = nc.tensor.matmul(sc[cp % 2][:, half * 512:(half + 1) * 512],
                                            k_stage[:, slot, c * P:(c + 1) * P], q_stage[:, slot, :],
                                            start=True, stop=True)
                last.then_inc(scores_ready, 1)

            def weigh(slot, cp):
                for two in range(2):
                    for half in range(2):
                        j = 2 * two + half
                        last = nc.tensor.matmul(
                            pj[slot][32 * j:32 * j + 2 * VW, 0:2 * P],
                            v_stage[:, slot, 2 * cp + half, two * 2 * VW:(two + 1) * 2 * VW],
                            probs[:, cp % 4, half * 512 + two * 256:half * 512 + (two + 1) * 256],
                            start=(cp == 0), stop=(cp == PAIRS - 1), tile_position=(0, 32 * j), skip_group_check=True)
                if cp == PAIRS - 1:
                    last.then_inc(av_ready, 1)

            def unit(n, slot, more=True, turn_last_keys=False):
                for cp in range(PAIRS):
                    pe.wait_ge(probs_ready, PAIRS * n + cp + 1)
                    if cp + 2 < PAIRS:
                        scores(slot, cp + 2)
                    elif more:
                        if cp + 2 == PAIRS:
                            pe.wait_ge(staged, n + 2)
                        scores(1 - slot, cp + 2 - PAIRS)
                    weigh(slot, cp)
                    if turn_last_keys and TURN_AT <= cp < TURN_AT + GRP:
                        turn_keys(1, GROUPS - 1, cp - TURN_AT)

            def merge(b):
                for g in range(NG):
                    n = UNITS.index((b, g))
                    pe.wait_ge(av_taken, n + 1)
                    for ab in range(2):
                        for half in range(2):
                            last = nc.tensor.matmul(
                                (turn_bank, av)[b][:, (2 * g + ab) * 2 * VW:(2 * g + ab + 1) * 2 * VW],
                                av_hl[:, n, half, ab * P:(ab + 1) * P],
                                pick[:, ab, :, :].rearrange("p t d -> p (t d)"), start=(half == 0), stop=(half == 1))
                last.then_inc(merged, 1)

            pe.wait_ge(kv_taken, CHUNKS)
            pe.wait_ge(sums_cleared, 1)
            pe.wait_ge(staged, 1)
            scores(0, 0)
            scores(0, 1)
            unit(0, 0, turn_last_keys=True)
            unit(1, 1)
            with pe.Fori(1, NG - 1) as i:
                for slot in range(2):
                    unit(2 * i + slot, slot)
            unit(2 * NG - 2, 0)
            merge(0)
            unit(2 * NG - 1, 1, more=False)
            merge(1)
            keep_warm(17)

            turn_h(2, h, h_ready, hT_turned)
            pe.wait_ge(hT_ready, 1)
            pe.wait_ge(attn_in, 7 * 16)
            for qk in (1, 0):
                for half in range(KT):
                    for kt in range(KT):
                        last = nc.tensor.matmul((self_q, self_k)[qk][half], wqk_sb[:, kt, KT * qk + half, :],
                                                hT[:, kt, :], start=(kt == 0), stop=(kt == KT - 1))
                    last.then_inc(qkv_ready, 1)

            def self_bank(u):
                return sc[u // 2 % 2][:, u % 2 * 512:(u % 2 + 1) * 512]

            def self_scores(u):
                b, s = u // SQ, u % SQ
                if u < 3:
                    pe.wait_ge(kbd_ready[u // 2], u % 2 + 1)
                    pe.wait_ge(qT_ready, min(u + 1, KT))
                if u >= 4:
                    pe.wait_ge(o_out, u - 3)
                nc.tensor.matmul(self_bank(u), qT[:, s // 2, b * P:(b + 1) * P],
                                 kbd[:, b, s // 2, s % 2 * 4:s % 2 * 4 + 4, :].rearrange("p j n -> p (j n)"),
                                 start=True, stop=True).then_inc(s_ready, 1)

            def self_turn(u):
                if u == 1:
                    pe.wait_ge(sv_ready, 1)
                pe.wait_ge(s_exp, u + 1)
                if u >= 2:
                    pe.wait_ge(pT_ready, u - 1)
                for j in range(4):
                    last = nc.tensor.transpose(pj[u % 2][:, j * P:(j + 1) * P], sprob[:, u % 2, j * P:(j + 1) * P],
                                               ident[:, :])
                last.then_inc(p_turned, 1)

            def self_weigh(u):
                b, s = u // SQ, u % SQ
                pe.wait_ge(pT_ready, u + 1)
                for j in range(4):
                    last = nc.tensor.matmul(self_bank(u)[32 * j:32 * j + SVW, 0:P], sv[:, b, 4 * s + j, :],
                                            sprobT[:, u % 2, j * P:(j + 1) * P], start=True, stop=True,
                                            tile_position=(0, 32 * j), skip_group_check=True)
                last.then_inc(o_ready, 1)

            def self_back(u):
                b, s = u // SQ, u % SQ
                pe.wait_ge(o_out, u + 1)
                nc.tensor.transpose((turn_bank, av)[b][:, s * P:(s + 1) * P], so[:, u % 2, :],
                                    ident[:, :]).then_inc(o_back, 1)

            units = B * SQ
            for b in range(B):
                last = rows(pj[1], b, wsv_sb, D, at=b * D)
                if b == B - 1:
                    last.then_inc(qkv_ready, 1)
                self_scores(b)
            for u in range(units + 2):
                if u < units:
                    self_turn(u)
                if u >= 2:
                    self_back(u - 2)
                if u + 2 < units:
                    self_scores(u + 2)
                if 1 <= u <= units:
                    self_weigh(u - 1)
                if u == units - 2:
                    keep_warm(3, sc[0])
                if u == units:
                    keep_warm(2, sc[0])
            keep_warm(4, sc[0])
            turn_h(1, h, o_norm, oT_turned)
            keep_warm(4, sc[1])
            pe.wait_ge(oT_ready, 1)
            for b in range(B):
                last = rows(pj[1], b, wout_sb, D, at=b * D)
            last.then_inc(y_ready, 1)

            keep_warm(16)

            turn_h(3, h, h_ready, hT_turned)
            pe.wait_ge(hT_ready, 2)
            for b in range(B):
                last = rows(turn_bank, b, gate_sb, E, at=b * E)
            last.then_inc(logits_ready, 1)

            def up(s, t, routed=True):
                slot = s % SLOTS
                pe.wait_ge(wlo_ready, t + 1)
                bank = sc[slot // 2][:, slot % 2 * 512:(slot % 2 + 1) * 512]
                for gu in range(2):
                    for kt in range(KT):
                        at = (gu * KT + kt) * P
                        for n, (wh, xh) in enumerate(HALVES):
                            last = nc.tensor.matmul(bank[:, gu * TOK:(gu + 1) * TOK], w_hl[:, s % RING, wh, at:at + P],
                                                    xT_hl[:, xh, kt, :], start=(kt == 0 and n == 0),
                                                    stop=(kt == KT - 1 and n == len(HALVES) - 1))
                if routed:
                    if not (isinstance(t, int) and t < 2):
                        pe.wait_ge(weighed, t - 1)
                    last = nc.tensor.matmul((turn_bank, av)[s % 2][:, 0:TOK], onehot[:, bass.ts(t - SHARED_TILES, P)],
                                            combT[:, :], start=True, stop=True)
                last.then_inc(up_ready, 1)

            def down(s, t):
                slot = s % SLOTS
                pe.wait_ge(alo_ready, t + 1)
                for b in range(B):
                    for n, (ah, wh) in enumerate(HALVES):
                        last = nc.tensor.matmul(pj[b][:, 0:D], act_hl[:, slot, ah, b * P:(b + 1) * P],
                                                w_hl[:, s % RING, wh, 2 * KT * P:TILE_W],
                                                start=(isinstance(t, int) and t == 0 and n == 0),
                                                stop=(isinstance(t, int) and t == TILES - 1 and n == len(HALVES) - 1),
                                                skip_group_check=True)
                last.then_inc(down_done, 1)

            pe.wait_ge(xlo_ready, 1)
            for t in range(SHARED_TILES):
                up(t, t, False)
            down(0, 0)
            pe.wait_ge(comb_ready, 1)
            for b in range(B):
                last = nc.tensor.transpose(av[:, :].bitcast(F16)[:, b * P:(b + 1) * P],
                                           comb_hl[:, b, :, :].rearrange("p t e -> p (t e)"), ident_h[:, :])
            last.then_inc(comb_turned, 1)
            pe.wait_ge(combT_ready, 1)
            pe.wait_ge(half_in, 16)
            pe.wait_ge(onehot_step, 3)
            up(3, 3)
            down(1, 1)
            for t in range(SLOTS, RING):
                up(t, t)
                down(t - 2, t - 2)
            with pe.Fori(0, TILES // RING - 1) as i:
                for s in range(RING):
                    up(s, RING * i + RING + s)
                    down(s - 2, RING * i + RING + s - 2)
            for t in range(TILES // RING * RING, TILES):
                up(t, t)
                down(t - 2, t - 2)
            down(TILES - 2, TILES - 2)
            down(TILES - 1, TILES - 1)

        @block.scalar
        def _(act):
            def take_kv(slot, grp, c):
                act.wait_ge(kv_ready, grp * GRP + c + 1)
                if c == 0 and not (isinstance(grp, int) and grp < 2):
                    act.wait_ge(normed, grp - 1)
                src, down = pj[c % 2], 1.0 / (CTX_UP * WKV_UP)
                nc.scalar.activation(ksq[:, slot, c * D:(c + 1) * D], src[:, 0:D], ACT.Square, scale=down)
                nc.scalar.activation(kraw[:, slot, c * D:(c + 1) * D], src[:, 0:D], ACT.Copy, scale=down)
                dst = v_all[:, :, bass.ds(grp * GRP + c, 1), :].rearrange(
                    "p g c (h d) -> p g (c h) d", h=4)[:, :, :, 0:XD]
                nc.scalar.activation(dst, src[:, D:2 * D].rearrange("p (g h d) -> p g h d", g=NG, h=4),
                                     ACT.Copy, scale=down).then_inc(kv_taken, 1)

            def take_keys(grp, c):
                act.wait_ge(turned, grp * GRP + c + 1)
                src = (turn_bank, av)[c % 2][:, :].bitcast(F16).rearrange("p (g n) -> p g n", g=NG)
                nc.scalar.activation(kT[:, :, bass.ts(grp * GRP + c, P)], src, ACT.Copy).then_inc(turn_free, 1)

            def roots(nth, n):
                act.wait_ge(sums_ready, nth)
                nc.scalar.activation(rs_x[:, 0:n], rs_h[:, 0:n], ACT.Sqrt, scale=1.0 / XD,
                                     bias=rms_eps).then_inc(roots_ready, 1)

            def load_table(n, function):
                nc.scalar.activation(table_out[:, n:n + 1], ln_eps, function)

            act.wait_ge(eps_set, 2)
            load_table(0, ACT.Sqrt)
            def ln_roots(nth, b0, n):
                act.wait_ge(sums_ready, nth)
                nc.scalar.activation(rs_x[:, 0:n], mv[:, b0:b0 + n, 1], ACT.Sqrt, bias=ln_eps).then_inc(roots_ready, 1)

            ln_roots(1, 0, B)
            act.wait_ge(wkv_in, 16)
            nc.scalar.activation(wkv_hl[:, 0, :, :], wkv_sb[:, :, :], ACT.Copy, scale=WKV_UP).then_inc(wkv_hi, 1)
            act.wait_ge(hT_turned, 1)
            nc.scalar.activation(hT[:, :, :].rearrange("p k t -> p (k t)"), sc[0][:, 0:512],
                                 ACT.Copy).then_inc(hT_first, 1)
            act.wait_ge(q_ready, 1)
            nc.scalar.activation(q_sq, sc[1][:, 0:B * D], ACT.Square)
            nc.scalar.activation(q_raw, sc[1][:, 0:B * D], ACT.Copy).then_inc(q_out, 1)
            act.wait_ge(ident_done, 2)
            for c in range(GRP):
                take_kv(0, 0, c)
                if c == 0:
                    roots(2, B * XH)
            for c in range(GRP):
                take_kv(1, 1, c)
                if c == 1:
                    roots(3, GRP * XH)

            def take_queries(b):
                act.wait_ge(q_turned, b + 1)
                src = (turn_bank, av)[b][:, :].bitcast(F16).rearrange("p (g n) -> p g n", g=NG)
                nc.scalar.activation(q_all[:, :, b, :], src, ACT.Copy).then_inc(q_taken, 1)

            for b in range(B):
                take_queries(b)

            def take_both(i):
                for slot in range(2):
                    for c in range(GRP):
                        take_kv(slot, 2 * i + slot, c)
                        take_keys(2 * i + slot - 2, c)
                        if c == 0:
                            roots(2 * i + slot + 2, GRP * XH)

            take_both(1)
            with act.Fori(2, GROUPS // 2) as i:
                take_both(i)
            for c in range(GRP):
                take_keys(GROUPS - 2, c)
                if c == 1:
                    roots(GROUPS + 2, GRP * XH)

            def exp_unit(n):
                for cp in range(PAIRS):
                    act.wait_ge(scores_ready, PAIRS * n + cp + 1)
                    nc.scalar.activation(probs[:, cp % 4, :], sc[cp % 2][:, :], ACT.Exp,
                                         scale=XD ** -0.5 / QK_UP ** 2).then_inc(probs_ready, 1)

            exp_unit(0)
            exp_unit(1)
            with act.Fori(1, NG) as i:
                for slot in range(2):
                    exp_unit(2 * i + slot)

            def split_hi(s, t, loads):
                act.wait_ge(moe_in[s % RING], loads)
                if not (isinstance(t, int) and t < RING):
                    act.wait_ge(down_done, t - RING + 1)
                nc.scalar.activation(w_hl[:, s % RING, 0, :], ring[:, s % RING, :], ACT.Copy, scale=W_UP).then_inc(whi_ready, 1)

            load_table(1, ACT.Sqrt)
            act.wait_ge(av_taken, 2 * NG)
            ln_roots(GROUPS + 3, B - 1, 1)
            load_table(2, ACT.Exp)
            for t in range(SLOTS):
                split_hi(t, t, 16)
            act.wait_ge(qkv_ready, 2)
            act.wait_ge(own_biased, 1)
            for j in range(P // SD):
                last = nc.scalar.activation(kbd[:, :, 1, j, :], self_k[1].rearrange("p (b n) -> p b n", b=B),
                                            ACT.Identity, scale=own_rows[:, j:j + 1], bias=own_bias[:, j:j + 1])
            last.then_inc(kbd_ready[1], 1)
            units = B * SQ

            def self_exp(u):
                act.wait_ge(s_topped, u + 1)
                if u >= 2:
                    act.wait_ge(p_turned, u - 1)
                for j in range(4):
                    at = u % 2 * 512 + j * P
                    last = nc.scalar.activation(sprob[:, u % 2, j * P:(j + 1) * P], sc[u // 2 % 2][:, at:at + P],
                                                ACT.Exp, bias=less_top[:, 4 * u + j:4 * u + j + 1])
                last.then_inc(s_exp, 1)

            def self_out(u):
                act.wait_ge(o_ready, u + 1)
                if u >= 2:
                    act.wait_ge(o_back, u - 1)
                at = u % 2 * 512
                nc.scalar.activation(so[:, u % 2, :], sc[u // 2 % 2][:, at:at + P], ACT.Copy).then_inc(o_out, 1)

            self_exp(0)
            for u in range(units + 2):
                if u >= 2:
                    self_out(u - 2)
                if u + 1 < units:
                    self_exp(u + 1)
            load_table(3, ACT.Sqrt)
            ln_roots(GROUPS + 4, 0, B)
            load_table(4, ACT.Exp)

            act.wait_ge(hT_ready, 2)
            nc.scalar.activation(xT_hl[:, 0, :, :], hT[:, :, :], ACT.Copy, scale=X_UP).then_inc(xhi_ready, 1)
            act.wait_ge(logits_shifted, 1)
            nc.scalar.activation(comb[:, :, :], comb[:, :, :], ACT.Exp).then_inc(gate_exp, 1)

            def silu(s, t):
                act.wait_ge(up_ready, t + 1)
                if not (isinstance(t, int) and t < 2):
                    act.wait_ge(weighed, t - 1)
                slot = s % SLOTS
                nc.scalar.activation(sil[:, s % 2, :], sc[slot // 2][:, slot % 2 * 512:slot % 2 * 512 + TOK],
                                     ACT.Silu, scale=1.0 / (W_UP * X_UP)).then_inc(sil_ready, 1)

            def split_act_hi(s, t):
                if not (isinstance(t, int) and t < SLOTS):
                    act.wait_ge(down_done, t - SLOTS + 1)
                act.wait_ge(weighed, t + 1)
                nc.scalar.activation(act_hl[:, s % SLOTS, 0, :], act_sb[:, s % 2, :], ACT.Copy).then_inc(ahi_ready, 1)

            for t in range(RING + 2):
                silu(t, t)
                if t + 2 >= SLOTS:
                    split_hi(t + 2, t + 2, 16 * (1 + (t + 2) // RING))
                split_act_hi(t, t)
            with act.Fori(1, TILES // RING - 1) as i:
                for s in range(2, 2 + RING):
                    silu(s, RING * i + s)
                    split_hi(s + 2, RING * i + s + 2, 16 * i + 16 * (1 + (s + 2) // RING))
                    split_act_hi(s, RING * i + s)
            for t in range((TILES // RING - 1) * RING + 2, TILES):
                silu(t, t)
                if t + 2 < TILES:
                    split_hi(t + 2, t + 2, 16 * (1 + (t + 2) // RING))
                split_act_hi(t, t)

        @block.vector
        def _(dve):
            step = Steps(dve, dve_step)
            v = nc.vector

            def newton_step(n):
                h_, t_, y_ = (a[:, 0:n] for a in (rs_h, rs_t, rs_y))
                for c in range(n):
                    step(v.scalar_tensor_tensor(out=t_[:, c:c + 1], in0=y_[:, c:c + 1], scalar=h_[:, c:c + 1],
                                                in1=y_[:, c:c + 1], op0=ALU.mult, op1=ALU.mult))
                step.wait()
                step.then(v.scalar_tensor_tensor(out=y_, in0=t_, scalar=1.5, in1=y_, op0=ALU.add, op1=ALU.mult))

            def newton_by_column(n):
                x_, h_, t_, y_ = (a[:, 0:n] for a in (rs_x, rs_h, rs_t, rs_y))
                step(v.tensor_scalar(h_, x_, -0.5, None, ALU.mult))
                step.then(v.tensor_scalar(t_.bitcast(U32), x_.bitcast(U32), 1, 0x7FFFFFFF,
                                          ALU.logical_shift_right, ALU.bitwise_xor))
                step.then(v.tensor_scalar(y_, t_, SEED, None, ALU.mult))
                for _ in range(3):
                    newton_step(n)

            def layernorm(batches=range(B), nth_root=None):
                b0, n = batches[0], len(batches)
                for b in batches:
                    step(v.bn_stats(stats[:, b, :], xres[:, b, :]))
                step.wait()
                if nth_root is not None:
                    for b in batches:
                        last = v.bn_aggr(mv[:, b, :], stats[:, b, :])
                    last.then_inc(sums_ready, 1)
                    dve.wait_ge(sums_ready, nth_root)
                    step(v.tensor_scalar(rs_h[:, 0:n], mv[:, b0:b0 + n, 1], LN_EPS, -0.5, ALU.add, ALU.mult))
                    dve.wait_ge(roots_ready, nth_root)
                    step.then(v.reciprocal(rs_y[:, 0:n], rs_x[:, 0:n]))
                    newton_step(n)
                else:
                    for b in batches:
                        step(v.bn_aggr(mv[:, b, :], stats[:, b, :]))
                    step.wait()
                    step.then(v.tensor_scalar(rs_x[:, 0:n], mv[:, b0:b0 + n, 1], LN_EPS, None, ALU.add))
                    newton_by_column(n)
                for b in batches:
                    last = v.tensor_scalar(h[:, b, :], xres[:, b, :], mv[:, b, 0:1], rs_y[:, b - b0:b - b0 + 1],
                                           ALU.subtract, ALU.mult)
                if b == B - 1:
                    last.then_inc(h_ready, 1)

            def take_hT(n, turned, ready):
                dve.wait_ge(turned, n)
                v.tensor_copy(hT[:, :, :].rearrange("p k t -> p (k t)"), sc[0][:, 0:512]).then_inc(ready, 1)

            def ask_roots(sq, heads):
                v.tensor_reduce(rs_h[:, 0:heads], sq.rearrange("p (h d) -> p h d", d=XD), AX,
                                ALU.add).then_inc(sums_ready, 1)

            def normalise(nth, raw, hi_lo, heads, lo_at):
                dve.wait_ge(roots_ready, nth)
                step.then(v.reciprocal(rs_y[:, 0:heads], rs_x[:, 0:heads]))
                n3 = kn[:, 0:heads * XD].rearrange("p (h d) -> p h d", d=XD)
                raw3 = raw.rearrange("p (h d) -> p h d", d=XD)
                parts = [slice(n * heads // 2, (n + 1) * heads // 2) for n in range(2)]
                for n, hs in enumerate(parts):
                    step(v.scalar_tensor_tensor(out=n3[:, hs, :], in0=raw3[:, hs, :], scalar=QK_UP,
                                                in1=rs_y[:, hs].unsqueeze(2).broadcast_to([P, heads // 2, XD]),
                                                op0=ALU.mult, op1=ALU.mult))
                for hs in parts:
                    step.wait_older(1)
                    step(v.tensor_copy(hi_lo[:, hs, 0:XD], n3[:, hs, :]))
                for hs in parts:
                    step.wait_older(1)
                    step(v.tensor_tensor(hi_lo[:, hs, lo_at:lo_at + XD], n3[:, hs, :], hi_lo[:, hs, 0:XD],
                                         ALU.subtract))
                return parts

            def may_split(slot, grp, loads):
                dve.wait_ge(ctx_in[slot], loads)
                if not (isinstance(grp, int) and grp < 2):
                    dve.wait_ge(kv_ready, GRP * (grp - 1))

            def split_ctx_hi(slot):
                src = ctx_in_sb[:, slot, :, :].rearrange("p k n -> p (k n)")
                step(v.tensor_scalar(ctx_hl[:, slot, 0, :], src, CTX_UP, None, ALU.mult))

            def split_ctx_lo(slot):
                src = ctx_in_sb[:, slot, :, :].rearrange("p k n -> p (k n)")
                v.scalar_tensor_tensor(out=ctx_hl[:, slot, 1, :], in0=src, scalar=CTX_UP, in1=ctx_hl[:, slot, 0, :],
                                       op0=ALU.mult, op1=ALU.subtract).then_inc(ctx_lo, 1)

            v.memset(ln_eps, LN_EPS).then_inc(eps_set, 1)
            v.memset(rms_eps, RMS_EPS).then_inc(eps_set, 1)
            dve.wait_ge(ident_done, 1)
            step(v.tensor_copy(ident_h[:, :], ident[:, :]))
            idv = ident[:, :].rearrange("p (t half n) -> p t half n", t=2, half=2)
            for ab in range(2):
                step(v.tensor_tensor(pick[:, ab, :, :], idv[:, :, 0, ab * VW:(ab + 1) * VW],
                                     idv[:, :, 1, ab * VW:(ab + 1) * VW], ALU.add))

            dve.wait_ge(x_in, 16)
            layernorm(nth_root=1)
            dve.wait_ge(wkv_hi, 1)
            v.scalar_tensor_tensor(out=wkv_hl[:, 1, :, :].rearrange("p k n -> p (k n)"),
                                   in0=wkv_sb[:, :, :].rearrange("p k n -> p (k n)"), scalar=WKV_UP,
                                   in1=wkv_hl[:, 0, :, :].rearrange("p k n -> p (k n)"),
                                   op0=ALU.mult, op1=ALU.subtract).then_inc(wkv_lo, 1)
            may_split(0, 0, 16)
            split_ctx_hi(0)
            step.wait()
            split_ctx_lo(0)
            may_split(1, 1, 16)
            split_ctx_hi(1)
            step.wait()
            split_ctx_lo(1)
            dve.wait_ge(q_out, 1)
            ask_roots(q_sq, B * XH)
            normalise(2, q_raw, q32, B * XH, 2 * XD)
            step.wait()
            q_halves = q32.rearrange("p h (half two d) -> p h half two d", half=2, two=2)
            v.tensor_copy(q_halves[:, :, :, 1, :], q_halves[:, :, :, 0, :]).then_inc(q_normed, 1)
            may_split(0, 2, 32)
            split_ctx_hi(0)
            step.wait()
            split_ctx_lo(0)

            def ask_key_roots(slot, grp):
                dve.wait_ge(kv_taken, GRP * grp + GRP)
                ask_roots(ksq[:, slot, :], GRP * XH)

            def normalise_keys(slot, grp):
                if grp >= 2:
                    dve.wait_ge(turned, GRP * grp - GRP)
                for hs in normalise(grp + 3, kraw[:, slot, :], k32[:, slot, :, :], GRP * XH, XD):
                    step.wait_older(1)
                    last = v.tensor_copy(k32[:, slot, hs, 2 * XD:], k32[:, slot, hs, 0:2 * XD])
                    if hs.stop < GRP * XH:
                        step(last)
                last.then_inc(normed, 1)

            def stage(slot, b, g):
                v.tensor_copy(k_stage[:, slot, :], kT[:, bass.ds(g, 1), b * CTX:(b + 1) * CTX].rearrange(
                    "p g n -> p (g n)"))
                v.tensor_copy(v_stage[:, slot, :, :].rearrange("p c n -> p (c n)"),
                              v_all[:, bass.ds(g, 1), b * CPB:(b + 1) * CPB, :].rearrange("p g c n -> p (g c n)"))
                for j in range(4):
                    rows = slice(32 * j, 32 * j + 32)
                    last = v.tensor_copy(q_stage[rows, slot, j * P:(j + 1) * P],
                                         q_all[rows, bass.ds(g, 1), b, :].rearrange("p g n -> p (g n)"))
                last.then_inc(staged, 1)

            for grp in range(GROUPS):
                if 0 < grp < GROUPS - 2:
                    may_split(grp % 2, grp + 2, 16 * (1 + (grp + 2) // 2))
                    split_ctx_hi(grp % 2)
                ask_key_roots(grp % 2, grp)
                if 0 < grp < GROUPS - 2:
                    step.wait()
                    split_ctx_lo(grp % 2)
                if grp == GROUPS - 1:
                    dve.wait_ge(q_taken, B)
                    dve.wait_ge(q_cleared, 1)
                    dve.wait_ge(turn_free, CPB)
                    stage(0, *UNITS[0])
                    for b in range(B):
                        last = v.memset(pj[b][:, :], 0.0)
                    last.then_inc(sums_cleared, 1)
                normalise_keys(grp % 2, grp)
            stage(1, *UNITS[1])

            def take_av(n, slot):
                dve.wait_ge(av_ready, n + 1)
                src, to = pj[slot][:, 0:2 * P], av_hl[:, bass.ds(n, 1), :, :]
                hi, lo = (to[:, :, half, :].rearrange("p u n -> p (u n)") for half in range(2))
                step.then(v.tensor_scalar(hi, src, AV_DOWN, None, ALU.mult))
                v.scalar_tensor_tensor(out=lo, in0=src, scalar=AV_DOWN, in1=hi, op0=ALU.mult,
                                       op1=ALU.subtract).then_inc(av_taken, 1)

            dve.wait_ge(attn_in, 7 * 16)
            dve.wait_ge(own_done, 3)
            v.tensor_scalar(own_bias[:, :], own_rows[:, :], bqk_sb[:, KT + 1:KT + 2], None,
                            ALU.mult).then_inc(own_biased, 1)
            dve.wait_ge(turn_free, CHUNKS - GRP)
            for c in range(GRP):
                dve.wait_ge(turned, CHUNKS - GRP + c + 1)
                at = CHUNKS - GRP + c
                v.tensor_copy(kT[:, :, at * P:(at + 1) * P], (turn_bank, av)[c % 2][:, :].bitcast(F16).rearrange(
                    "p (g n) -> p g n", g=NG)).then_inc(last_taken, 1)
            dve.wait_ge(last_taken, GRP)
            with dve.Fori(0, NG - 2) as i:
                step.enter(i, 0, B)
                take_av(2 * i, 0)
                stage(0, 1, i)
                take_av(2 * i + 1, 1)
                stage(1, 0, i + 2)
            step.leave(NG - 2)
            for n in range(2 * NG - 4, 2 * NG - 2):
                take_av(n, n % 2)
                stage(n % 2, *UNITS[n + 2])
            take_av(2 * NG - 2, 0)

            for b in range(B):
                if b == B - 1:
                    take_av(2 * NG - 1, 1)
                dve.wait_ge(merged, b + 1)
                got = (turn_bank, av)[b][:, 0:XH * VW].rearrange("p (g ab t d) -> p g t ab d", g=NG, ab=2, t=2)
                rec = srec[:, b, :].rearrange("p (g t ab) -> p g t ab", g=NG, t=2)
                step.then(v.reciprocal(rec, got[:, :, :, :, XD]))
                new = h[:, b, :].rearrange("p (g t ab d) -> p g t ab d", g=NG, t=2, ab=2)
                for ab in range(2):
                    step(v.tensor_tensor(new[:, :, :, ab, :], got[:, :, :, ab, 0:XD],
                                         rec[:, :, :, ab].unsqueeze(3).broadcast_to([P, NG, 2, XD]), ALU.mult))
                step.wait()
                step.then(v.tensor_tensor(xres[:, b, :], xres[:, b, :], h[:, b, :], ALU.add))
                layernorm(range(b, b + 1), nth_root=GROUPS + 3 if b == B - 1 else None)

            take_hT(2, hT_turned, hT_ready)
            def split_lo(s, t):
                dve.wait_ge(whi_ready, t + 1)
                v.scalar_tensor_tensor(out=w_hl[:, s % RING, 1, :], in0=ring[:, s % RING, :], scalar=W_UP,
                                       in1=w_hl[:, s % RING, 0, :], op0=ALU.mult, op1=ALU.subtract).then_inc(wlo_ready, 1)

            step(v.tensor_tensor(xres[:, :, :], xres[:, :, :], bout_sb[:, :].unsqueeze(1).broadcast_to([P, B, D]),
                                 ALU.add))
            v.memset(sv[:, :, :, SD:SVW], 1.0)
            dve.wait_ge(qkv_ready, 1)
            for j in range(P // SD):
                last = v.tensor_scalar(kbd[:, :, 0, j, :], self_k[0].rearrange("p (b n) -> p b n", b=B),
                                       bqk_sb[:, KT:KT + 1], own_rows[:, j:j + 1], ALU.add, ALU.mult)
                if j in (3, 7):
                    last.then_inc(kbd_ready[0], 1)
                if j == 5:
                    dve.wait_ge(qkv_ready, 4)
                    for half in range(KT):
                        v.tensor_scalar(qT[:, half, :], self_q[half], bqk_sb[:, half:half + 1], SD ** -0.5,
                                        ALU.add, ALU.mult).then_inc(qT_ready, 1)

            def self_tops(u):
                dve.wait_ge(s_ready, u + 1)
                src = sc[u // 2 % 2][:, u % 2 * 512:(u % 2 + 1) * 512].rearrange("p (h n) -> p h n", h=4)
                v.tensor_reduce(less_top[:, 4 * u:4 * u + 4], src, AX, ALU.max, negate=True).then_inc(s_topped, 1)

            def self_take_turned(u):
                dve.wait_ge(p_turned, u + 1)
                if u >= 2:
                    dve.wait_ge(o_ready, u - 1)
                v.tensor_copy(sprobT[:, u % 2, :], pj[u % 2][:, :]).then_inc(pT_ready, 1)

            def self_norm(b):
                dve.wait_ge(o_back, SQ * (b + 1))
                got = (turn_bank, av)[b][:, :].rearrange("p (h d) -> p h d", d=32)
                step.then(v.reciprocal(srec[:, b, 0:SH], got[:, :, SD]))
                return v.tensor_tensor(h[:, b, :].rearrange("p (h d) -> p h d", d=SD), got[:, :, 0:SD],
                                       srec[:, b, 0:SH].unsqueeze(2).broadcast_to([P, SH, SD]), ALU.mult)

            units = B * SQ
            self_tops(0)
            for u in range(units):
                if u + 1 < units:
                    self_tops(u + 1)
                if u == 0:
                    dve.wait_ge(qkv_ready, 5)
                    v.tensor_tensor(sv[:, :, :, 0:SD], pj[1][:, :].rearrange("p (b h d) -> p b h d", b=B, h=SH),
                                    bv_sb[:, :].rearrange("p (h d) -> p h d", h=SH).unsqueeze(1).broadcast_to([P, B, SH, SD]),
                                    ALU.add).then_inc(sv_ready, 1)
                self_take_turned(u)
                if u == SQ + 2:
                    step(self_norm(0))
            split_lo(0, 0)
            self_norm(1).then_inc(o_norm, 1)
            take_hT(1, oT_turned, oT_ready)
            for t in range(1, SHARED_TILES):
                split_lo(t, t)
            dve.wait_ge(y_ready, 1)
            xflat = xres[:, :, :].rearrange("p b n -> p (b n)")
            step.then(v.tensor_tensor(xflat, xflat, pj[1][:, :], ALU.add))

            def gate_up(s, t, routed=True):
                slot = s % SLOTS
                upv = sc[slot // 2][:, slot % 2 * 512 + TOK:(slot % 2 + 1) * 512]
                dve.wait_ge(sil_ready, t + 1)
                share = COMB_UP if routed else 1.0
                to = gated if routed else act_sb
                first = v.scalar_tensor_tensor(out=to[:, s % 2, :], in0=upv, scalar=ACT_UP / (W_UP * X_UP * share),
                                               in1=sil[:, s % 2, :], op0=ALU.mult, op1=ALU.mult)
                if routed:
                    step.then(first)
                    v.tensor_tensor(act_sb[:, s % 2, :], gated[:, s % 2, :], (turn_bank, av)[s % 2][:, 0:TOK],
                                    ALU.mult).then_inc(weighed, 1)
                else:
                    first.then_inc(weighed, 1)

            def split_act_lo(s, t):
                slot = s % SLOTS
                dve.wait_ge(ahi_ready, t + 1)
                v.tensor_tensor(act_hl[:, slot, 1, :], act_sb[:, s % 2, :], act_hl[:, slot, 0, :],
                                ALU.subtract).then_inc(alo_ready, 1)

            layernorm(nth_root=GROUPS + 4)
            take_hT(3, hT_turned, hT_ready)
            step(v.memset(ppad[:, :, E:E + 1], -1.0))
            step(v.memset(ppad[:, :, E + 1:E + 2], -2.0))
            step(v.memset(topk[:, :, TOPK:TOPK + 1], -1.0))
            step(v.memset(topk[:, :, TOPK + 1:TOPK + 2], -2.0))
            split_lo(SHARED_TILES, SHARED_TILES)
            dve.wait_ge(xhi_ready, 1)
            v.scalar_tensor_tensor(out=xT_hl[:, 1, :, :].rearrange("p k t -> p (k t)"),
                                   in0=hT[:, :, :].rearrange("p k t -> p (k t)"), scalar=X_UP,
                                   in1=xT_hl[:, 0, :, :].rearrange("p k t -> p (k t)"),
                                   op0=ALU.mult, op1=ALU.subtract).then_inc(xlo_ready, 1)

            def over_experts(a):
                return a.unsqueeze(2).broadcast_to([P, B, E])

            dve.wait_ge(logits_ready, 1)
            lg = turn_bank[:, 0:B * E].rearrange("p (b e) -> p b e", b=B)
            top, total, part = rstat[:, 0, :], rstat[:, 1, :], rstat[:, 2, :]
            p_in = ppad[:, :, 0:E]
            step.then(v.tensor_reduce(top, lg, AX, ALU.max))
            v.tensor_tensor(comb[:, :, :], lg, over_experts(top), ALU.subtract).then_inc(logits_shifted, 1)
            dve.wait_ge(gate_exp, 1)
            step.then(v.tensor_reduce(total, comb[:, :, :], AX, ALU.add))
            step.then(v.reciprocal(total, total))
            step.then(v.tensor_tensor(p_in, comb[:, :, :], over_experts(total), ALU.mult))
            for b in range(B):
                step(v.max(top8[:, b, :], ppad[:, b, :]))
            step.wait()
            step.then(v.tensor_copy(topk[:, :, 0:TOPK], top8[:, :, 0:TOPK]))
            step(v.tensor_reduce(part, topk[:, :, 0:TOPK], AX, ALU.add))
            for b in range(B):
                step(v.match_replace(out=prep[:, b, :], in_to_replace=topk[:, b, :], in_values=ppad[:, b, :],
                                     imm_value=-3.0))
            gate_up(0, 0, False)
            step.wait()
            step(v.tensor_scalar(part, part, TOPK_EPS, 1.0 / COMB_UP, ALU.add, ALU.mult))
            step.then(v.tensor_tensor(prep[:, :, 0:E], p_in, prep[:, :, 0:E], ALU.not_equal))
            step(v.reciprocal(part, part))
            split_act_lo(0, 0)
            step.then(v.tensor_tensor(prep[:, :, 0:E], p_in, prep[:, :, 0:E], ALU.mult))
            step.then(v.tensor_tensor(comb[:, :, :], prep[:, :, 0:E], over_experts(part), ALU.mult))
            step.then(v.tensor_copy(comb_hl[:, :, 0, :], comb[:, :, :]))
            v.tensor_tensor(comb_hl[:, :, 1, :], comb[:, :, :], comb_hl[:, :, 0, :],
                            ALU.subtract).then_inc(comb_ready, 1)
            dve.wait_ge(comb_turned, 1)
            v.tensor_copy(combT[:, :], av[:, :].bitcast(F16)[:, 0:TOK]).then_inc(combT_ready, 1)

            for t in range(1, RING + 2):
                gate_up(t, t, t >= SHARED_TILES)
                if t + 2 >= SLOTS:
                    split_lo(t + 2, t + 2)
                split_act_lo(t, t)
            with dve.Fori(1, TILES // RING - 1) as i:
                step.enter(i, 1, RING)
                for s in range(2, 2 + RING):
                    gate_up(s, RING * i + s)
                    split_lo(s + 2, RING * i + s + 2)
                    split_act_lo(s, RING * i + s)
            step.leave(TILES // RING - 2)
            for t in range((TILES // RING - 1) * RING + 2, TILES):
                gate_up(t, t)
                if t + 2 < TILES:
                    split_lo(t + 2, t + 2)
                split_act_lo(t, t)
            dve.wait_ge(down_done, TILES)
            for b in range(B):
                last = v.scalar_tensor_tensor(out=final[:, b, :], in0=pj[b][:, 0:D], scalar=1.0 / (W_UP * ACT_UP),
                                              in1=xres[:, b, :], op0=ALU.mult, op1=ALU.add)
            last.then_inc(final_ready, 1)


def kernel(**inputs):
    import numpy as np
    import concourse.bacc as bacc
    from concourse.bass_utils import run_bass_kernel_spmd

    a = {k: np.asarray(v) for k, v in inputs.items()}

    def kparts(w):
        return np.ascontiguousarray(w.reshape(KT, P, -1).transpose(1, 0, 2))

    arrays = {"x": np.ascontiguousarray(a["x"].transpose(1, 0, 2))}
    arrays["ctxT"] = kparts(a["ctx_2048"].reshape(B * CTX, D).T)
    arrays["wq"] = kparts(a["L0_xattn_Wq"].T)
    w = np.concatenate([a["L0_xattn_Wk"], a["L0_xattn_Wv"]]).reshape(D, 2, D)
    arrays["wkv"] = kparts(np.concatenate([w[:, 0].T, w[:, 1].T], axis=1))
    wqkv = a["L0_attn_W_qkv"].reshape(D, SH, 3, SD)
    bqkv = a["L0_attn_b_qkv"].reshape(SH, 3, SD)
    arrays["wqk"] = kparts(wqkv[:, :, :2].transpose(0, 2, 1, 3).reshape(D, -1)).reshape(P, KT, 2 * KT, P)
    arrays["bqk"] = np.ascontiguousarray(bqkv[:, :2].transpose(1, 0, 2).reshape(2 * KT, P).T)
    arrays["wsv"] = kparts(wqkv[:, :, 2].reshape(D, D))
    arrays["bv"] = np.ascontiguousarray(bqkv[:, 2].reshape(1, D))
    arrays["wout"] = kparts(a["L0_attn_W_out"])
    arrays["bout"] = a["L0_attn_b_out"].reshape(1, D)
    arrays["gate"] = kparts(a["L0_ffn_gate_w"].T)
    gu, dn = a["L0_ffn_w_gate_up"], a["L0_ffn_w_down"]
    sgu, sdn = a["L0_ffn_ws_gate_up"], a["L0_ffn_ws_down"]
    moe = np.zeros((TILES, P, TILE_W), gu.dtype)
    for n, (routed, shared) in enumerate(((gu[:, :FFN], sgu[:2 * FFN]), (gu[:, FFN:], sgu[2 * FFN:]))):
        rows = np.zeros((TILES * P, D), gu.dtype)
        rows[:2 * FFN] = shared
        rows[SHARED_TILES * P:] = routed.reshape(-1, D)
        moe[:, :, n * KT * P:(n + 1) * KT * P] = rows.reshape(TILES, P, KT, P).transpose(0, 3, 2, 1).reshape(
            TILES, P, KT * P)
    rows = np.zeros((TILES * P, D), gu.dtype)
    rows[:2 * FFN] = sdn.T
    rows[SHARED_TILES * P:] = dn.transpose(0, 2, 1).reshape(-1, D)
    moe[:, :, 2 * KT * P:] = rows.reshape(TILES, P, D)
    arrays["moe"] = moe

    nc = bacc.Bacc("TRN2", target_bir_lowering=False, num_devices=1)
    order = ["x", "ctxT", "wq", "wkv", "wqk", "wsv", "bqk", "bv", "wout", "bout", "gate", "moe"]
    args = [nc.dram_tensor(f"{n}_dram", arrays[n].shape, F32, kind="ExternalInput").ap() for n in order]
    out = nc.dram_tensor("out_dram", (P, B, D), F32, kind="ExternalOutput").ap()
    perceiver(nc, *args, out)
    r = run_bass_kernel_spmd(nc, [{f"{n}_dram": arrays[n] for n in order}], core_ids=[0])
    return np.ascontiguousarray(r.results[0]["out_dram"].transpose(1, 0, 2))
```
